# Optimizing a Trainium2 kernel written in Bass

```python
import numpy as np
import jax
import jax.numpy as jnp

def _softmax(x, axis=-1):
    return jax.nn.softmax(x, axis=axis)

def _gelu(x):
    return jax.nn.gelu(x, approximate=True)

def _silu(x):
    return jax.nn.silu(x)

def _sigmoid(x):
    return jax.nn.sigmoid(x)

def _layernorm(x, axis=-1, eps=1e-05):
    m = jnp.mean(x, axis=axis, keepdims=True)
    v = jnp.var(x, axis=axis, keepdims=True)
    return (x - m) / jnp.sqrt(v + eps)

def _scatter_add(tgt, idx, src, axis=0):
    return tgt.at[idx].add(src)

def _segment_sum(src, seg, n):
    return jax.ops.segment_sum(src, seg, n)
kernel_name = 'mk_decoder_postln_d1_seqx_r8_3428fa'

def setup_inputs(seed: int=0):
    np.random.seed(seed)
    _w = jnp.asarray

    def _rec_inputs():
        import jax
        import jax.numpy as jnp
        _rk = jax.random.key(seed)
        x = -0.0005207 + 1.001 * jax.random.normal(jax.random.fold_in(_rk, 1), (128, 64, 128), jnp.float32)
        _lenS = 64 - jax.random.randint(jax.random.fold_in(_rk, 7), (128,), 0, max(1, 64 // 4) + 1, jnp.int32)
        _lenS2 = 64 - jax.random.randint(jax.random.fold_in(_rk, 8), (128,), 0, max(1, 64 // 4) + 1, jnp.int32)
        _ctx_512P = jax.random.normal(jax.random.fold_in(_rk, 11), (128, 16, 64), jnp.float32)
        _ctx_512c = jax.random.dirichlet(jax.random.fold_in(_rk, 511), 0.3 * jnp.ones((16,), jnp.float32), (128, 64))
        _ctx_512t = jnp.einsum('bsk,bkd->bsd', _ctx_512c, _ctx_512P)
        _ctx_512t = _ctx_512t * jax.lax.rsqrt(jnp.mean(jnp.square(_ctx_512t)) + 1e-12) * 0.953939
        ctx_512 = 0.502058 + 0.29099 * (_ctx_512t + 0.3 * jax.random.normal(jax.random.fold_in(_rk, 611), (128, 64, 64), jnp.float32))
        itok_BxS2xS_0_7 = jax.random.randint(jax.random.fold_in(_rk, 12), (128, 64, 64), 0, 8, jnp.int32)
        return (x, ctx_512, itok_BxS2xS_0_7)
    x, ctx_512, itok_BxS2xS_0_7 = _rec_inputs()

    def _L0_attn_setup():
        import jax, jax.numpy as jnp
        import numpy as np
        import math
        D_MODEL = 128
        N_HEADS = 16
        HEAD_DIM = D_MODEL // N_HEADS
        FACTOR = 5
        B, L = (4, 512)
        key = jax.random.key(seed)
        ks = jax.random.split(key, 10)
        s = 1.0 / math.sqrt(D_MODEL)
        U = min(FACTOR * int(math.ceil(math.log(L))), L)
        return {'x': jax.random.normal(ks[0], (B, L, D_MODEL), dtype=jnp.float32), 'Wq': jax.random.normal(ks[1], (D_MODEL, D_MODEL), dtype=jnp.float32) * s, 'bq': jnp.zeros((D_MODEL,), jnp.float32), 'Wk': jax.random.normal(ks[2], (D_MODEL, D_MODEL), dtype=jnp.float32) * s, 'bk': jnp.zeros((D_MODEL,), jnp.float32), 'Wv': jax.random.normal(ks[3], (D_MODEL, D_MODEL), dtype=jnp.float32) * s, 'bv': jnp.zeros((D_MODEL,), jnp.float32), 'Wo': jax.random.normal(ks[4], (D_MODEL, D_MODEL), dtype=jnp.float32) * s, 'bo': jnp.zeros((D_MODEL,), jnp.float32), 'sample_idx': jax.random.permutation(ks[5], L)[:U].astype(jnp.int32)}
    _L0_attn_all = _L0_attn_setup()
    _L0_attn_in = {k: v for k, v in _L0_attn_all.items() if k in ('Wq', 'bq', 'Wk', 'bk', 'Wv', 'bv', 'Wo', 'bo', 'sample_idx')}
    del _L0_attn_all

    def _L0_xattn_setup():
        import jax, jax.numpy as jnp
        import numpy as np
        key = jax.random.key(seed)
        k1, k2, k3, k4, k5 = jax.random.split(key, 5)
        B, K, S, E, I, D = (4, 2, 64, 8, 128, 256)
        x = jax.random.normal(k1, (B, S, I), dtype=jnp.float32)
        weights = jax.random.uniform(k2, (B, K, S), dtype=jnp.float32)
        ensembles = jax.random.randint(k3, (B, K, S), 0, E, dtype=jnp.int64)
        lim1 = float(np.sqrt(6.0 / (D + I)))
        proj_in = jax.random.uniform(k4, (E, D, I), dtype=jnp.float32, minval=-lim1, maxval=lim1)
        proj_out = jax.random.uniform(k5, (E, I, D), dtype=jnp.float32, minval=-lim1, maxval=lim1)
        return {'x': x, 'weights': weights, 'ensembles': ensembles, 'proj_in': proj_in, 'proj_out': proj_out}
    _L0_xattn_all = _L0_xattn_setup()
    _L0_xattn_in = {k: v for k, v in _L0_xattn_all.items() if k in ('proj_in', 'proj_out')}
    del _L0_xattn_all

    def _L0_ffn_setup():
        import jax, jax.numpy as jnp
        import numpy as np
        B, S, D = (2, 256, 128)
        E, K, F = (16, 2, 64)
        FS = 128
        key = jax.random.key(seed)
        ks = jax.random.split(key, 8)

        def w(k, shape, fan_in):
            return jax.random.normal(k, shape, jnp.float32) / np.sqrt(fan_in).astype(np.float32)
        return {'x': jax.random.normal(ks[0], (B, S, D), jnp.float32), 'Wr': w(ks[1], (D, E), D), 'Wg': w(ks[2], (E, D, F), D), 'Wu': w(ks[3], (E, D, F), D), 'Wd': w(ks[4], (E, F, D), F), 'Sg': w(ks[5], (D, FS), D), 'Su': w(ks[6], (D, FS), D), 'Sd': w(ks[7], (FS, D), FS)}
    _L0_ffn_all = _L0_ffn_setup()
    _L0_ffn_in = {k: v for k, v in _L0_ffn_all.items() if k in ('Wr', 'Wg', 'Wu', 'Wd', 'Sg', 'Su', 'Sd')}
    del _L0_ffn_all
    return {'x': x, 'ctx_512': ctx_512, 'itok_BxS2xS_0_7': itok_BxS2xS_0_7, 'L0_attn_Wq': _L0_attn_in['Wq'], 'L0_attn_bq': _L0_attn_in['bq'], 'L0_attn_Wk': _L0_attn_in['Wk'], 'L0_attn_bk': _L0_attn_in['bk'], 'L0_attn_Wv': _L0_attn_in['Wv'], 'L0_attn_bv': _L0_attn_in['bv'], 'L0_attn_Wo': _L0_attn_in['Wo'], 'L0_attn_bo': _L0_attn_in['bo'], 'L0_attn_sample_idx': _L0_attn_in['sample_idx'], 'L0_xattn_proj_in': _L0_xattn_in['proj_in'], 'L0_xattn_proj_out': _L0_xattn_in['proj_out'], 'L0_ffn_Wr': _L0_ffn_in['Wr'], 'L0_ffn_Wg': _L0_ffn_in['Wg'], 'L0_ffn_Wu': _L0_ffn_in['Wu'], 'L0_ffn_Wd': _L0_ffn_in['Wd'], 'L0_ffn_Sg': _L0_ffn_in['Sg'], 'L0_ffn_Su': _L0_ffn_in['Su'], 'L0_ffn_Sd': _L0_ffn_in['Sd']}

def reference(x, ctx_512, itok_BxS2xS_0_7, L0_attn_Wq, L0_attn_bq, L0_attn_Wk, L0_attn_bk, L0_attn_Wv, L0_attn_bv, L0_attn_Wo, L0_attn_bo, L0_attn_sample_idx, L0_xattn_proj_in, L0_xattn_proj_out, L0_ffn_Wr, L0_ffn_Wg, L0_ffn_Wu, L0_ffn_Wd, L0_ffn_Sg, L0_ffn_Su, L0_ffn_Sd):
    import jax
    import jax.numpy as jnp

    def _L0_attn_ref(x, Wq, bq, Wk, bk, Wv, bv, Wo, bo, sample_idx):
        import jax, jax.numpy as jnp
        import numpy as np
        import math
        D_MODEL = 128
        N_HEADS = 16
        HEAD_DIM = D_MODEL // N_HEADS
        FACTOR = 5
        B, L = (4, 512)
        Bv, Lv, _ = x.shape
        scale = HEAD_DIM ** (-0.5)
        U = min(FACTOR * int(math.ceil(math.log(Lv))), Lv)

        def proj(W, b):
            y = jnp.einsum('bld,de->ble', x, W) + b
            return y.reshape(Bv, Lv, N_HEADS, HEAD_DIM).transpose(0, 2, 1, 3)
        Q = proj(Wq, bq)
        K = proj(Wk, bk)
        V = proj(Wv, bv)
        K_sample = K[:, :, sample_idx, :]
        QK_s = jnp.einsum('bhld,bhsd->bhls', Q, K_sample) * scale
        M = QK_s.max(axis=-1) - QK_s.mean(axis=-1)
        _, top_idx = jax.lax.top_k(M, U)
        Q_red = jnp.take_along_axis(Q, top_idx[..., None], axis=2)
        scores = jnp.einsum('bhud,bhld->bhul', Q_red, K) * scale
        attn = jax.nn.softmax(scores, axis=-1)
        out_red = jnp.einsum('bhul,bhld->bhud', attn, V)
        out = jnp.broadcast_to(V.mean(axis=2, keepdims=True), (Bv, N_HEADS, Lv, HEAD_DIM))
        bi = jnp.arange(Bv)[:, None, None]
        hi = jnp.arange(N_HEADS)[None, :, None]
        out = out.at[bi, hi, top_idx].set(out_red)
        out = out.transpose(0, 2, 1, 3).reshape(Bv, Lv, D_MODEL)
        return jnp.einsum('bld,de->ble', out, Wo) + bo

    def _L0_xattn_ref(x, weights, ensembles, proj_in, proj_out):
        import jax, jax.numpy as jnp
        import numpy as np
        E = proj_in.shape[0]
        h = jax.nn.relu(jnp.einsum('edi,bsi->bsed', proj_in, x))
        o = jnp.einsum('eid,bsed->bsei', proj_out, h)
        onehot = jax.nn.one_hot(ensembles, E, dtype=x.dtype)
        gate = jnp.einsum('bks,bkse->bse', weights, onehot)
        return jnp.einsum('bsei,bse->bsi', o, gate)

    def _L0_ffn_ref(x, Wr, Wg, Wu, Wd, Sg, Su, Sd):
        import jax, jax.numpy as jnp
        import numpy as np
        B, S, D = (2, 256, 128)
        E, K, F = (16, 2, 64)
        FS = 128
        b, s, d = x.shape
        T = b * s
        xf = x.reshape(T, d)
        shared = jax.nn.silu(xf @ Sg) * (xf @ Su) @ Sd
        probs = jax.nn.softmax(xf @ Wr, axis=-1)
        topk_p, topk_i = jax.lax.top_k(probs, K)
        n_exp = Wr.shape[1]
        cw = jnp.zeros((T, n_exp), x.dtype).at[jnp.arange(T)[:, None], topk_i].add(topk_p)

        def step(acc, ew):
            wg, wu, wd, c = ew
            y = jax.nn.silu(xf @ wg) * (xf @ wu) @ wd
            return (acc + y * c[:, None], None)
        routed, _ = jax.lax.scan(step, jnp.zeros_like(xf), (Wg, Wu, Wd, cw.T))
        return (routed + shared).reshape(b, s, d)
    x = _layernorm(x + _L0_attn_ref(x, L0_attn_Wq, L0_attn_bq, L0_attn_Wk, L0_attn_bk, L0_attn_Wv, L0_attn_bv, L0_attn_Wo, L0_attn_bo, L0_attn_sample_idx), axis=-1)
    x = _layernorm(x + _L0_xattn_ref(x, ctx_512, itok_BxS2xS_0_7, L0_xattn_proj_in, L0_xattn_proj_out), axis=-1)
    x = _layernorm(x + _L0_ffn_ref(x, L0_ffn_Wr, L0_ffn_Wg, L0_ffn_Wu, L0_ffn_Wd, L0_ffn_Sg, L0_ffn_Su, L0_ffn_Sd), axis=-1)
    return x

_drawn_inputs = setup_inputs


def setup_inputs(seed=0):
    import zlib

    import numpy as np

    out = dict(_drawn_inputs(seed))
    spreads = {'L0_attn_bq': (0.0, 0.1),
     'L0_attn_bk': (0.0, 0.1),
     'L0_attn_bv': (0.0, 0.1),
     'L0_attn_bo': (0.0, 0.1)}
    factors = {}
    for name, (base, spread) in spreads.items():
        noise = np.random.default_rng([zlib.crc32(name.encode()), seed]).standard_normal(out[name].shape)
        drawn = base * np.exp(spread * noise) if base else spread * noise
        out[name] = jnp.asarray(drawn.astype(out[name].dtype))
    for name, factor in factors.items():
        out[name] = (out[name] * factor).astype(out[name].dtype)
    return out
```

```python
from contextlib import ExitStack

import concourse.bass as bass
from concourse import mybir

F32 = mybir.dt.float32
F32R = mybir.dt.float32r
F16 = mybir.dt.float16
BF16 = mybir.dt.bfloat16
I32 = mybir.dt.int32
U32 = mybir.dt.uint32
ALU = mybir.AluOpType
ACT = mybir.ActivationFunctionType
X_AXIS = mybir.AxisListType.X

P = 128
B = 128
L = 64
D = 128
H = 16
HD = D // H
NS = 35
NTOP = 25
TC = 4
BC = 2 * TC
CW = TC * P
NCH = B // BC
UNITS = 2 * TC
KW = L + NS + 2
SW = L + NS + 1
SCALE = float(HD) ** -0.5
BIG = 3.0e38
EPS = 1e-5


def wait(engine, semaphore, value):
    if isinstance(value, int) and value <= 0:
        return
    engine.wait_ge(semaphore, value)


class Own:

    def __init__(self, engine, semaphore):
        self.engine, self.semaphore, self.n = engine, semaphore, 0

    def add(self, instruction):
        self.n += 1
        return instruction.then_inc(self.semaphore, 1)

    def settle(self):
        self.engine.wait_ge(self.semaphore, self.n)

    def restart(self):
        self.settle()
        self.engine.sem_clear(self.semaphore)
        self.n = 0


SLOTS = [
    ["A xT", "A xS"],
    ["F mT", "A q"],
    ["A k0", "A k1"],
    ["F sel", "A sq0", "A sq1"],
    ["A sq2", "A sq3"],
    ["F aT", "A sk00", "A sk01", "A sk10"],
    ["F y", "A sk11", "A sk20", "A sk21", "A sk30"],
    ["A sk31", "A v", "A vm", "F x1T"],
]


class Plan:

    def __init__(self, slots):
        self.slots = slots
        every = [n for s in slots for n in s]
        self.items = {"A": [n for n in every if n[0] == "A"], "F": [n for n in every if n[0] == "F"], "AF": every}
        assert len(every) % 2 == 0

    def at(self, c, name):
        a, f, af = (self.items[i] for i in ("A", "F", "AF"))
        if isinstance(c, int) and c <= 0:
            n = (c + 1) * len(a) + a.index(name)
            return n % 2, n // 2 + 1
        if isinstance(c, int) and c >= NCH - 1:
            n = 2 * len(a) + len(af) * (NCH - 2) + (c - NCH + 1) * len(f) + f.index(name)
            return n % 2, n // 2 + 1
        n = af.index(name)
        return n % 2, (c - 1) * (len(af) // 2) + len(a) + n // 2 + 1

    def now(self, u, prepare, finish):
        return [n for n in self.slots[u] if (prepare if n[0] == "A" else finish)]


ATTENTION = Plan(SLOTS)
spare_bank = ATTENTION.at


def loads_of(c, par):
    return 16 * c + 32 - 16 * par


def run_bodies(engine, body):
    body(-1, 1, scores=False, prepare=True, finish=False)
    body(0, 0, scores=True, prepare=True, finish=False)
    with engine.Fori(0, (NCH - 2) // 2) as pair:
        body(2 * pair + 1, 1, scores=True, prepare=True, finish=True)
        body(2 * pair + 2, 0, scores=True, prepare=True, finish=True)
    body(NCH - 1, 1, scores=True, prepare=False, finish=True)
    body(NCH, 0, scores=False, prepare=False, finish=True)


def attention(nc, k, x, wq, bq, wk, bk, wv, bv, wo, bo, sample_idx):
    with ExitStack() as ctx:
        def sb(name, shape, dt=F32):
            return ctx.enter_context(nc.sbuf_tensor(name, shape, dt))

        def ps(name, shape, dt=F32):
            return ctx.enter_context(nc.psum_tensor(name, shape, dt))

        def sem(name):
            return ctx.enter_context(nc.semaphore(name))

        X, XTh, XTl, ident = k.X, k.XTh, k.XTl, k.ident

        Wq, Wk, Wv, Wo = (sb(n, [P, D]) for n in ("Wq", "Wk", "Wv", "Wo"))
        Wqs = sb("Wqs", [P, D])
        bqc, bkc, bqs = sb("bqc", [P, 1]), sb("bkc", [P, 1]), sb("bqs", [P, 1])
        bvf = sb("bvf", [P, D])
        bvh = sb("bvh", [P, H // 2, HD])
        bof = sb("bof", [P, D])
        idx = sb("idx", [P, NS], I32)
        idf, neg = sb("idf", [P, NS]), sb("neg", [P, NS])
        lrow = sb("lrow", [P, 1], I32)
        lrowf = sb("lrowf", [P, 1])
        hot, cnt = sb("hot", [P, NS]), sb("cnt", [P, 1])
        SELW = NS + 2
        selbd = sb("selbd", [P, 2, SELW])
        rep = sb("rep", [P, 4, 4, P], F16)
        xin = sb("xin", [P, 2, TC, D])
        xb = sb("xb", [P, 2, TC, D])
        xT = sb("xT", [P, BC, KW])
        qhi, qlo = sb("qhi", [P, BC, L], F16), sb("qlo", [P, BC, L], F16)
        khi, klo = sb("khi", [P, BC, KW], F16), sb("klo", [P, BC, KW], F16)
        QS = sb("QS", [P, 2, 4, BC, L], F16)
        KS = sb("KS", [P, 2, 4, BC, SW], F16)
        VB = sb("VB", [P, 2, BC, H // 2, 2 * (HD + 1)])
        att = sb("att", [P, 2, TC, D])
        nmax, smax = sb("nmax", [P, 2, 8]), sb("smax", [P, 2, 8])
        PR = sb("PR", [P, 2, 8, L])
        PT = sb("PT", [P, 2, 4, P])
        M = sb("M", [P, 2, TC * H])
        NSENT = 8 * ((NTOP + 7) // 8) - NTOP
        top0, top1 = sb("top0", [P, L + NSENT]), sb("top1", [P, L + NSENT])
        mx8 = sb("mx8", [P, 8])
        freeing = sb("freeing", [1, 1])
        chosen = sb("chosen", [P, L])
        selT = sb("selT", [P, TC * H])
        O9 = sb("O9", [P, 2, TC, H, HD + 1])
        rden = sb("rden", [P, TC, H])
        onorm = sb("onorm", [P, TC, H, HD])
        attT = sb("attT", [P, CW])
        y = sb("y", [P, TC, D])
        stats, mv = sb("stats", [P, TC, 6]), sb("mv", [P, TC, 2])
        vare, rstd = sb("vare", [P, TC, 1]), sb("rstd", [P, TC, 1])
        x1s = sb("x1s", [P, TC, D])

        psS = [ps(f"psS{i}", [P, 2, 512]) for i in range(2)]
        psP = ps("psP", [P, 4, P])
        psO = ps("psO", [P, H * (HD + 1)])
        spare = [ps(f"spare{i}", [P, 512]) for i in range(2)]

        loaded = sem("weights_loaded")
        consts = sem("constants_made")
        folded = sem("constants_folded")
        x_loaded = [sem(f"x_loaded{i}") for i in range(2)]
        xb_made = sem("x_plus_bias_made")
        filled = [sem(f"spare{i}_filled") for i in range(2)]
        emptied = [sem(f"spare{i}_emptied") for i in range(2)]
        hi_made = sem("high_parts_made")
        scored = sem("scores_filled")
        scores_read = sem("scores_read")
        shifted = sem("scores_shifted")
        probs = sem("probabilities_made")
        turned = sem("probabilities_turned")
        turned_kept = sem("turned_probabilities_in_sbuf")
        weighed = sem("values_weighed")
        out_read = sem("output_tile_read")
        chosen_made = sem("choice_made")
        mixed = sem("heads_mixed")
        var_made = sem("variance_made")
        rstd_made = sem("rstd_made")
        x1_made = sem("x1_made")
        x1_kept = sem("x1_kept")
        hi_kept = sem("x1_high_part_kept")
        own_v = sem("vector_results")

        block = ctx.enter_context(nc.Block())

        @block.sync
        def _(sp):
            for dst, src in ((Wq, wq), (Wk, wk), (Wv, wv), (Wo, wo)):
                sp.dma_start(dst[:], src).then_inc(loaded, 16)
            sp.dma_start(bqc[:], bq.rearrange("(e a) -> e a", a=1)).then_inc(loaded, 16)
            sp.dma_start(bkc[:], bk.rearrange("(e a) -> e a", a=1)).then_inc(loaded, 16)
            sp.dma_start(bvf[:], bv.partition_broadcast(P)).then_inc(loaded, 16)
            sp.dma_start(bof[:], bo.partition_broadcast(P)).then_inc(loaded, 16)
            sp.dma_start(idx[:], sample_idx.partition_broadcast(P)).then_inc(loaded, 16)

            def load(c, par):
                for b2 in range(2):
                    src = x[bass.ds(BC * c, BC)].rearrange("(t b) l d -> b l t d", b=2)
                    sp.dma_start(xin[L * b2:L * b2 + L, par], src[b2]).then_inc(x_loaded[par], 16)

            load(0, 0)
            load(1, 1)
            with sp.Fori(0, (NCH - 2) // 2) as pair:
                sp.wait_ge(xb_made, 2 * pair + 1)
                load(2 * pair + 2, 0)
                sp.wait_ge(xb_made, 2 * pair + 2)
                load(2 * pair + 3, 1)

        @block.gpsimd
        def _(pool):
            pool.iota(lrow[0:L], pattern=[[0, 1]], base=0, channel_multiplier=1).then_inc(consts, 1)
            pool.wait_ge(consts, 1)
            pool.iota(lrow[L:P], pattern=[[0, 1]], base=0, channel_multiplier=1).then_inc(consts, 1)
            pool.wait_ge(consts, 2)
            pool.memset(rep[:], 0.0).then_inc(consts, 1)
            pool.memset(selbd[:], 0.0).then_inc(consts, 1)
            pool.memset(VB[:], 0.0).then_inc(consts, 1)
            pool.memset(top0[:], BIG).then_inc(consts, 1)
            pool.memset(rstd[:], 0.0).then_inc(x1_kept, 1)
            pool.wait_ge(consts, 6)
            for half in range(2):
                pool.memset(VB[L * half:L * half + L, :, :, :, (HD + 1) * half + HD], 1.0).then_inc(consts, 1)
                pool.wait_ge(consts, 7 + half)
            for kind, (k0, k1) in enumerate(((0, 1), (2, 3), (0, 2), (1, 3))):
                for t in range(4):
                    v = rep[:, kind, t].rearrange("p (j k d) -> p j k d", j=4, k=4)[:, :, k0:k1 + 1:k1 - k0, :]
                    pool.affine_select(out=v, in_=v, compare_op=ALU.not_equal, fill=1.0, base=-HD * t,
                                       pattern=[[-32, 4], [0, 2], [-1, HD]], channel_multiplier=1
                                       ).then_inc(consts, 1)

            def body(c, par, scores, prepare, finish):
                n = 1 - par
                if finish:
                    pool.wait_ge(var_made, c)
                    pool.tensor_tensor(rstd[:], vare[:], k.minus_half[:, 0:TC, :], ALU.pow).then_inc(rstd_made, 1)
                    pool.wait_ge(x1_made, c)
                    pool.tensor_copy(X[:, bass.ds((c - 1) * TC, TC), :], x1s[:]).then_inc(x1_kept, 1)
                if prepare:
                    pool.wait_ge(x_loaded[n], loads_of(c + 1, n))
                    b, m = spare_bank(c, "A xS")
                    pool.wait_ge(emptied[b], m)
                    bias = bof[:].rearrange("p (a d) -> p a d", a=1).to_broadcast([P, TC, D])
                    pool.tensor_tensor(xb[:, n], xin[:, n], bias, ALU.add).then_inc(xb_made, 1)

            pool.wait_ge(loaded, 16 * 9)
            run_bodies(pool, body)
            pool.wait_ge(x1_kept, NCH + 1)

        @block.tensor
        def _(pe):
            pe.wait_ge(consts, 24)
            pe.wait_ge(folded, 10)
            pe.wait_ge(loaded, 16 * 9)

            def body(c, par, scores, prepare, finish):
                nxt = prv = 1 - par

                def kept(name):
                    b, n = spare_bank(c, name)
                    pe.wait_ge(emptied[b], n)

                def item(name):
                    b, n = spare_bank(c, name)
                    bank = spare[b]
                    wait(pe, emptied[b], n - 1)
                    if name == "A xT":
                        pe.wait_ge(x_loaded[nxt], loads_of(c + 1, nxt))
                        for t in range(TC):
                            last = pe.transpose(bank[:, P * t:P * t + P], xin[:, nxt, t], ident[:])
                    elif name == "A xS":
                        for t in range(TC):
                            last = pe.matmul(bank[:, 2 * SELW * t:2 * SELW * (t + 1)], xin[:, nxt, t],
                                             selbd[:].rearrange("p b s -> p (b s)"), start=True, stop=True)
                    elif name == "A q":
                        kept("A xT")
                        kept("A xS")
                        last = pe.matmul(bank[:], Wqs[:], xT[:, :, 0:L], start=True, stop=True)
                    elif name in ("A k0", "A k1"):
                        h = int(name[-1])
                        last = pe.matmul(bank[:, 0:4 * KW], Wk[:],
                                         xT[:, 4 * h:4 * h + 4, :].rearrange("p b s -> p (b s)"),
                                         start=True, stop=True)
                    elif name == "A v":
                        wvh = Wv[:].rearrange("p (a b d) -> p a b d", b=2, d=HD)
                        for n in range(BC):
                            for hh in range(2):
                                last = pe.matmul(bank[L * hh:L * hh + L, L * n:L * n + L], xT[:, n, 0:L],
                                                 wvh[:, :, hh, :], start=True, stop=True)
                    elif name == "A vm":
                        for n in range(BC):
                            mean = xT[:, n, KW - 1:KW].to_broadcast([P, L])
                            last = pe.matmul(bank[L * (n % 2):L * (n % 2) + L, P * (n // 2):P * (n // 2) + P],
                                             mean, Wv[:], start=True, stop=True)
                    elif name[:4] == "A sq":
                        t = int(name[4])
                        kept("A q")
                        pe.matmul(bank[:], rep[:, 0, t], qhi[:].rearrange("p b l -> p (b l)"), start=True, stop=False)
                        last = pe.matmul(bank[:], rep[:, 1, t], qlo[:].rearrange("p b l -> p (b l)"),
                                         start=False, stop=True)
                    elif name[:4] == "A sk":
                        t, h = int(name[4]), int(name[5])
                        kept("A k1")
                        kept("A k0")
                        pe.matmul(bank[:, 0:4 * SW], rep[:, 2, t], khi[:, 4 * h:4 * h + 4, 0:SW],
                                  start=True, stop=False)
                        last = pe.matmul(bank[:, 0:4 * SW], rep[:, 3, t], klo[:, 4 * h:4 * h + 4, 0:SW],
                                         start=False, stop=True)
                    elif name == "F mT":
                        pe.wait_ge(scores_read, UNITS * c)
                        last = pe.matmul(bank[0:TC * H, 0:P], M[:, prv], ident[:], start=True, stop=True)
                    elif name == "F sel":
                        pe.wait_ge(chosen_made, c)
                        last = pe.matmul(bank[0:L, 0:P], chosen[:], ident[:], start=True, stop=True)
                    elif name == "F aT":
                        pe.wait_ge(mixed, c)
                        for t in range(TC):
                            last = pe.transpose(bank[:, P * t:P * t + P], att[:, prv, t], ident[:])
                    elif name == "F y":
                        kept("F aT")
                        for t in range(TC):
                            last = pe.matmul(bank[:, P * t:P * t + P], attT[:, P * t:P * t + P], Wo[:],
                                             start=True, stop=True)
                    elif name == "F x1T":
                        pe.wait_ge(x1_made, c)
                        for t in range(TC):
                            last = pe.transpose(bank[:, P * t:P * t + P], x1s[:, t], ident[:])
                    last.then_inc(filled[b], 1)

                def score(u):
                    t, jp = u // 2, u % 2
                    if u == 0:
                        if isinstance(c, int) and c == 0:
                            for name in ("A sk30", "A sk31"):
                                b, n = spare_bank(-1, name)
                                pe.wait_ge(emptied[b], n)
                        else:
                            pe.wait_ge(turned_kept, UNITS * c - 1)
                    wait(pe, scores_read, UNITS * c + u - 1)
                    for tt in range(4):
                        for jj in range(2):
                            for b2 in range(2):
                                j, b = 2 * jp + jj, 2 * t + b2
                                last = pe.matmul(psS[u % 2][L * b2:L * b2 + L, jj, SW * tt:SW * (tt + 1)],
                                                 QS[32 * j:32 * j + 32, par, tt, b, :],
                                                 KS[32 * j:32 * j + 32, par, tt, b, :], start=True, stop=True)
                    last.then_inc(scored, 1)

                def turn(u):
                    g = UNITS * c + u - 1
                    pe.wait_ge(probs, g + 1)
                    wait(pe, turned_kept, g)
                    for q in range(4):
                        last = pe.transpose(psP[:, q], PR[:, (u - 1) % 2, 2 * q:2 * q + 2, :].rearrange("p a l -> p (a l)"),
                                            ident[:])
                    last.then_inc(turned, 1)

                def weigh(u):
                    v, vp = (u - 2) % UNITS, par if u >= 2 else prv
                    t, jp = v // 2, v % 2
                    pe.wait_ge(turned_kept, UNITS * c + u - 1)
                    if jp == 0:
                        wait(pe, out_read, TC * c + (u - 2) // 2)
                    for q in range(4):
                        for b2 in range(2):
                            last = pe.matmul(
                                psO[L * b2:L * b2 + L, 18 * (4 * jp + q):18 * (4 * jp + q + 1)],
                                PT[:, v % 2, q, L * b2:L * b2 + L], VB[:, vp, 2 * t + b2, 4 * jp + q, :],
                                start=True, stop=True)
                    last.then_inc(weighed, 1)

                for u in range(UNITS):
                    if scores:
                        score(u)
                    for name in ATTENTION.now(u, prepare, finish):
                        item(name)
                    if (scores and u >= 1) or (u == 0 and finish):
                        turn(u)
                    if (scores and u >= 2) or (u < 2 and finish):
                        weigh(u)

            run_bodies(pe, body)

        @block.scalar
        def _(act):
            act.wait_ge(folded, 10)
            act.wait_ge(loaded, 16 * 9)

            def body(c, par, scores, prepare, finish):
                nxt = 1 - par

                def item(name):
                    if name in ("A v", "A vm", "F mT", "F sel", "F y"):
                        return
                    b, n = spare_bank(c, name)
                    bank = spare[b]
                    act.wait_ge(filled[b], n)
                    if name == "A xT":
                        act.copy(xT[:, :, 0:L], bank[:].rearrange("p (b l) -> p b l", l=L)).then_inc(emptied[b], 1)
                    elif name == "A xS":
                        act.copy(xT[:, :, L:KW], bank[:, 0:BC * SELW].rearrange("p (b s) -> p b s", s=SELW)
                                 ).then_inc(emptied[b], 1)
                    elif name == "A q":
                        act.activation(qhi[:], bank[:].rearrange("p (b l) -> p b l", l=L), ACT.Identity,
                                       bias=bqs[:, 0:1]).then_inc(hi_made, 1)
                    elif name in ("A k0", "A k1"):
                        h = int(name[-1])
                        act.activation(khi[:, 4 * h:4 * h + 4], bank[:, 0:4 * KW].rearrange("p (b s) -> p b s", s=KW),
                                       ACT.Identity, bias=bkc[:, 0:1]).then_inc(hi_made, 1)
                    elif name[:4] == "A sq":
                        act.copy(QS[:, nxt, int(name[4])], bank[:].rearrange("p (b l) -> p b l", l=L)
                                 ).then_inc(emptied[b], 1)
                    elif name[:4] == "A sk":
                        t, h = int(name[4]), int(name[5])
                        act.copy(KS[:, nxt, t, 4 * h:4 * h + 4], bank[:, 0:4 * SW].rearrange("p (b s) -> p b s", s=SW)
                                 ).then_inc(emptied[b], 1)
                    elif name == "F aT":
                        act.copy(attT[:], bank[:]).then_inc(emptied[b], 1)
                    elif name == "F x1T":
                        act.copy(XTh[:, bass.ds((c - 1) * CW, CW)], bank[:]).then_inc(hi_kept, 1)

                for u in range(UNITS):
                    for name in ATTENTION.now(u, prepare, finish):
                        item(name)
                    g = UNITS * c + u
                    if (scores and u >= 1) or (u == 0 and finish):
                        act.wait_ge(turned, g)
                        wait(act, weighed, g - 2)
                        act.copy(PT[:, (u - 1) % 2], psP[:]).then_inc(turned_kept, 1)
                    if scores:
                        act.wait_ge(shifted, g + 1)
                        act.activation(PR[:, u % 2], PR[:, u % 2], ACT.Exp).then_inc(probs, 1)

            run_bodies(act, body)

        @block.vector
        def _(dve):
            own = Own(dve, own_v)
            tt, ts, stt = dve.tensor_tensor, dve.tensor_scalar, dve.scalar_tensor_tensor
            dve.wait_ge(loaded, 16 * 9)
            dve.wait_ge(consts, 24)
            ts(Wqs[:], Wq[:], SCALE, None, ALU.mult).then_inc(folded, 1)
            ts(bqs[:], bqc[:], SCALE, None, ALU.mult).then_inc(folded, 1)
            bvp = bvf[:].rearrange("p (a b d) -> p a b d", b=2, d=HD)
            for half in range(2):
                dve.tensor_copy(bvh[L * half:L * half + L], bvp[L * half:L * half + L, :, half, :]).then_inc(folded, 1)
            own.add(dve.tensor_copy(idf[:], idx[:]))
            own.add(dve.tensor_copy(lrowf[:], lrow[:]))
            own.settle()
            own.add(ts(neg[:], idf[:], 0.0, float(L), ALU.is_lt, ALU.mult))
            own.settle()
            own.add(tt(idf[:], idf[:], neg[:], ALU.add))
            own.settle()
            own.add(ts(idf[:], idf[:], 0.0, float(L - 1), ALU.max, ALU.min))
            own.settle()
            own.add(ts(hot[:], idf[:], lrowf[:, 0:1], None, ALU.is_equal))
            own.settle()
            own.add(dve.reduce_sum(cnt[:], hot[:], axis=X_AXIS))
            own.settle()
            for half in range(2):
                rows = slice(L * half, L * half + L)
                dve.tensor_copy(selbd[rows, half, 0:NS], hot[rows]).then_inc(folded, 1)
                ts(selbd[rows, half, NS:NS + 1], cnt[rows], 1.0 / NS, None, ALU.mult).then_inc(folded, 1)
                dve.memset(selbd[rows, half, NS + 1:NS + 2], 1.0 / L).then_inc(folded, 1)
            own.restart()

            def body(c, par, scores, prepare, finish):
                nxt = prv = 1 - par

                def unit(u):
                    s = psS[u % 2][:, :, 0:4 * SW].rearrange("p j (t k) -> p j t k", t=4)
                    dve.wait_ge(scored, UNITS * c + u + 1)
                    nm = nmax[:, u % 2].rearrange("p (j t a) -> p j t a", j=2, a=1)
                    sm = smax[:, u % 2].rearrange("p (j t a) -> p j t a", j=2, a=1)
                    own.add(dve.tensor_reduce(nm[:, :, :, 0], s[:, :, :, 0:L], X_AXIS, ALU.max, negate=True))
                    own.add(dve.tensor_reduce(sm[:, :, :, 0], s[:, :, :, L:L + NS], X_AXIS, ALU.max))
                    own.settle()
                    wait(dve, turned, UNITS * c + u - 1)
                    pr = PR[:, u % 2].rearrange("p (j t) l -> p j t l", j=2)
                    tt(pr, s[:, :, :, 0:L], nm.to_broadcast([P, 2, 4, L]), ALU.add).then_inc(shifted, 1)
                    m = M[:, par, 8 * u:8 * u + 8].rearrange("p (j t) -> p j t", j=2)
                    tt(m, sm[:, :, :, 0], s[:, :, :, SW - 1], ALU.subtract).then_inc(scores_read, 1)

                def read_out(u):
                    tile = (u - 4) // 2 % TC
                    dve.wait_ge(weighed, UNITS * c + u - 2)
                    dve.tensor_copy(O9[:, par if u >= 4 else prv, tile].rearrange("p h d -> p (h d)"),
                                    psO[:]).then_inc(out_read, 1)

                def low(name):
                    b, n = spare_bank(c, name)
                    dve.wait_ge(hi_made, 3 * (c + 1) + 1 + ("A q", "A k0", "A k1").index(name))
                    if name == "A q":
                        stt(qlo[:], spare[b][:].rearrange("p (b l) -> p b l", l=L), bqs[:, 0:1], qhi[:],
                            ALU.add, ALU.subtract).then_inc(emptied[b], 1)
                    else:
                        h = int(name[-1])
                        stt(klo[:, 4 * h:4 * h + 4], spare[b][:, 0:4 * KW].rearrange("p (b s) -> p b s", s=KW),
                            bkc[:, 0:1], khi[:, 4 * h:4 * h + 4], ALU.add, ALU.subtract).then_inc(emptied[b], 1)

                def took(name):
                    b, n = spare_bank(c, name)
                    dve.wait_ge(filled[b], n)
                    return spare[b], emptied[b]

                def choose():
                    bank, done = took("F mT")
                    own.add(dve.tensor_copy(top0[0:L, 0:L], bank[0:L, 0:L]))
                    own.add(dve.tensor_copy(top0[L:P, 0:L], bank[0:L, L:P]))
                    dve.tensor_copy(freeing[:], bank[0:1, 0:1]).then_inc(done, 1)
                    own.settle()
                    src = top0
                    for r in range((NTOP + 7) // 8):
                        own.add(dve.max(mx8[:], src[:]))
                        own.settle()
                        own.add(dve.match_replace(top1[:], mx8[:], src[:], -BIG))
                        own.settle()
                        src = top1
                    ts(chosen[:], top1[:, 0:L], -BIG, None, ALU.is_le).then_inc(chosen_made, 1)

                def mix():
                    bank, done = took("F sel")
                    own.add(dve.tensor_copy(selT[0:L], bank[0:L, 0:L]))
                    own.add(dve.tensor_copy(selT[L:P], bank[0:L, L:P]))
                    dve.tensor_copy(freeing[:], bank[0:1, 0:1]).then_inc(done, 1)
                    dve.wait_ge(out_read, TC * c)
                    own.add(dve.reciprocal(rden[:], O9[:, prv, :, :, HD]))
                    own.settle()
                    r = rden[:].rearrange("p t (h a) -> p t h a", a=1).to_broadcast([P, TC, H, HD])
                    own.add(tt(onorm[:], O9[:, prv, :, :, 0:HD], r, ALU.mult))
                    own.settle()
                    mask = selT[:].bitcast(U32).rearrange("p (h a) -> p h a", a=1).to_broadcast([P, TC * H, HD])
                    dve.copy_predicated(att[:, prv].rearrange("p t (h d) -> p (t h) d", d=HD), mask,
                                        onorm[:].rearrange("p t h d -> p (t h) d")).then_inc(mixed, 1)

                def residual():
                    bank, done = took("F y")
                    dve.wait_ge(xb_made, c)
                    tt(y[:], bank[:].rearrange("p (t d) -> p t d", t=TC), xb[:, prv], ALU.add).then_inc(done, 1)
                    b, n = spare_bank(c, "F y")
                    dve.wait_ge(emptied[b], n)
                    for t in range(TC):
                        own.add(dve.bn_stats(stats[:, t], y[:, t]))
                    own.settle()
                    for t in range(TC):
                        own.add(dve.bn_aggr(mv[:, t], stats[:, t]))
                    own.settle()
                    ts(vare[:], mv[:, :, 1:2], EPS, None, ALU.add).then_inc(var_made, 1)

                def normalize():
                    dve.wait_ge(rstd_made, c)
                    dve.wait_ge(x1_kept, c)
                    for t in range(TC):
                        last = ts(x1s[:, t], y[:, t], mv[:, t, 0:1], rstd[:, t], ALU.subtract, ALU.mult)
                    last.then_inc(x1_made, 1)

                def values():
                    bank, done = took("A v")
                    for half in range(2):
                        r = slice(L * half, L * half + L)
                        last = tt(VB[r, nxt, :, :, (HD + 1) * half:(HD + 1) * half + HD],
                                  bank[r].rearrange("p (b h d) -> p b h d", b=BC, d=HD),
                                  bvh[r].rearrange("p (a h) d -> p a h d", a=1).to_broadcast([L, BC, H // 2, HD]),
                                  ALU.add)
                    last.then_inc(done, 1)
                    bank, done = took("A vm")
                    tt(att[:, nxt], bank[:].rearrange("p (t d) -> p t d", t=TC),
                       bvf[:].rearrange("p (a d) -> p a d", a=1).to_broadcast([P, TC, D]), ALU.add).then_inc(done, 1)

                def keep_low():
                    b, n = spare_bank(c, "F x1T")
                    dve.wait_ge(hi_kept, c)
                    chunk = bass.ds((c - 1) * CW, CW)
                    tt(XTl[:, chunk], spare[b][:], XTh[:, chunk].bitcast(F32), ALU.subtract).then_inc(emptied[b], 1)

                for u in range(UNITS):
                    if u % 2 == 0 and ((scores and u >= 4) or (finish and u <= 2)):
                        read_out(u)
                    if scores:
                        unit(u)
                    if u == 1 and finish:
                        choose()
                    if u == 1 and prepare:
                        low("A q")
                    if u == 2 and prepare:
                        low("A k0")
                        low("A k1")
                    if u == 3 and finish:
                        mix()
                    if u == 6 and finish:
                        residual()
                    if u == 7 and finish:
                        normalize()
                    if u == 7 and prepare:
                        values()
                    if u == 7 and finish:
                        keep_low()
                if own.n:
                    own.restart()

            run_bodies(dve, body)


E1, HID1 = 8, 256
U1 = E1 * HID1 // P
E2, F2 = 16, 64
LAG1 = 3
GATED = Plan([[], [], [], [], ["F oT"], [], [], [], ["F xT"], [], ["A sum"], ["F rt"], ["A gT"], [], ["F cT"], []])
PIECE = 4


def gated_experts(nc, k, ctx_w, itok, w_in, w_out, wr):
    with ExitStack() as ctx:
        def sb(name, shape, dt=F32):
            return ctx.enter_context(nc.sbuf_tensor(name, shape, dt))

        def ps(name, shape, dt=F32):
            return ctx.enter_context(nc.psum_tensor(name, shape, dt))

        def sem(name):
            return ctx.enter_context(nc.semaphore(name))

        X, XTh, XTl, ident, CWT = k.X, k.XTh, k.XTl, k.ident, k.CWT
        stage = sb("stage", [P, 4, PIECE, P])
        Wih, Wil = sb("Wih", [P, U1, P], F32R), sb("Wil", [P, U1, P], F32R)
        Woh, Wol = sb("Woh", [P, U1, P], F32R), sb("Wol", [P, U1, P], F32R)
        Wr = sb("Wr", [P, E2])
        identb = sb("identb", [P, P], BF16)
        halves = sb("halves", [P, 2])
        pick = sb("pick", [3 * E1, E1, P], BF16)
        wts, ids = sb("wts", [P, 2, TC, L]), sb("ids", [P, 2, TC, L], I32)
        wm, wm_done = sb("wm", [P, E1, TC, L]), sb("wm_done", [1, 1])
        freeing = sb("freeing2", [1, 1])
        g3 = sb("g3", [P, BC, 3, E1], BF16)
        gr = sb("gr", [L, BC, E1])
        GT = sb("GT", [3 * E1, 2, CW], BF16)
        rr, hg = sb("rr", [P, 2, CW]), sb("hg", [P, 2, CW])
        hh, hl = sb("hh", [P, 4, CW], F32R), sb("hl", [P, 4, CW], F32R)
        oT = sb("oT", [P, CW])
        y, x2s = sb("y2", [P, TC, D]), sb("x2s", [P, TC, D])
        stats, mv = sb("stats2", [P, TC, 6]), sb("mv2", [P, TC, 2])
        vare, rstd = sb("vare2", [P, TC, 1]), sb("rstd2", [P, TC, 1])
        x2T = sb("x2T", [P, CW])
        lmax, lsum, lrec = sb("lmax", [P, TC, 1]), sb("lsum", [P, TC]), sb("lrec", [P, TC, 1])
        lg = sb("lg", [P, TC, E2])
        pr0, pr1 = sb("pr0", [P, TC, E2 + 6]), sb("pr1", [P, TC, E2 + 6])
        mx8 = sb("mx8b", [P, TC, 8])
        cw, cwr = sb("cw", [P, TC, E2]), sb("cwr", [P, TC, E2])
        cw3 = sb("cw3", [P, TC, 3, E2], BF16)

        psH = [ps(f"psH{i}", [P, 512]) for i in range(2)]
        psG = [ps(f"psG{i}", [P, 512]) for i in range(2)]
        psO = [ps(f"psOut{i}", [P, 512]) for i in range(2)]
        spare = [ps(f"aux{i}", [P, 512]) for i in range(2)]

        loaded = sem("router_loaded")
        staged = [sem(f"weights_staged{i}") for i in range(4)]
        w_hi = sem("weights_high_made")
        w_lo = sem("weights_low_made")
        consts = sem("constants_made2")
        own_v, own_p = sem("vector_results2"), sem("pool_results2")
        gates_loaded = [sem(f"gates_loaded{i}") for i in range(2)]
        masked = sem("gates_masked")
        gates_made = sem("gates_made")
        filled = [sem(f"aux{i}_filled") for i in range(2)]
        emptied = [sem(f"aux{i}_emptied") for i in range(2)]
        hidden = sem("hidden_filled")
        rectified = sem("hidden_rectified")
        spread = sem("gate_spread")
        gated = sem("hidden_gated")
        hi_made = sem("hidden_high_made")
        lo_made = sem("hidden_low_made")
        added = sem("unit_added")
        oT_kept = sem("output_in_sbuf")
        var_made = sem("variance_made2")
        rstd_made = sem("rstd_made2")
        x2_made = sem("x2_made")
        x2_kept = sem("x2_kept")
        xh_kept = sem("x2_high_kept")
        shifted = sem("logits_shifted")
        raised = sem("logits_raised")
        routed = sem("routed")

        block = ctx.enter_context(nc.Block())
        pieces = [(w, i) for i in range(U1 // PIECE) for w in (0, 1)]

        @block.sync
        def _(sp):
            for n, (w, i) in enumerate(pieces):
                if n >= 4:
                    sp.wait_ge(w_lo, n - 3)
                src = (w_in, w_out)[w]
                sp.dma_start(stage[:, n % 4], src[:, PIECE * i:PIECE * (i + 1), :]).then_inc(staged[n % 4], 16)
            sp.dma_start(Wr[:], wr).then_inc(loaded, 16)

            def load(c, par):
                for src, dst in ((ctx_w, wts), (itok, ids)):
                    for b2 in range(2):
                        part = src[bass.ds(BC * c, BC)].rearrange("(t b) k s -> b k t s", b=2)[b2]
                        sp.dma_start(dst[L * b2:L * b2 + L, par], part).then_inc(gates_loaded[par], 16)

            load(0, 0)
            load(1, 1)
            with sp.Fori(0, (NCH - 2) // 2) as pair:
                sp.wait_ge(masked, 2 * pair + 1)
                load(2 * pair + 2, 0)
                sp.wait_ge(masked, 2 * pair + 2)
                load(2 * pair + 3, 1)

        @block.gpsimd
        def _(pool):
            pool.memset(g3[:], 0.0).then_inc(consts, 1)
            pool.memset(halves[:], 0.0).then_inc(consts, 1)
            pool.memset(pr0[:], BIG).then_inc(consts, 1)
            pool.memset(pick[:], 0.0).then_inc(consts, 1)
            pool.tensor_copy(identb[:], ident[:]).then_inc(consts, 1)
            pool.memset(rstd[:], 0.0).then_inc(x2_kept, 1)
            pool.wait_ge(consts, 5)
            for half in range(2):
                pool.memset(halves[L * half:L * half + L, half:half + 1], 1.0).then_inc(consts, 1)
                pool.wait_ge(consts, 6 + half)
            for part in range(3):
                pool.affine_select(out=pick[:], in_=pick[:], compare_op=ALU.not_equal, fill=1.0, base=-E1 * part,
                                   pattern=[[-1, E1], [0, P]], channel_multiplier=1).then_inc(consts, 1)
                pool.wait_ge(consts, 8 + part)
            pool.memset(CWT[:], 0.0).then_inc(consts, 1)
            own = Own(pool, own_p)

            def body(c, par, scores, prepare, finish):
                n = 1 - par
                if prepare:
                    pool.wait_ge(gates_loaded[n], 2 * loads_of(c + 1, n))
                    wait(pool, gates_made, c + 1)
                    own.add(pool.tensor_tensor(wm_done[:], k.minus_half[0:1, 0], k.minus_half[0:1, 0], ALU.add))
                    own.settle()
                    for e in range(E1):
                        own.add(pool.tensor_scalar(wm[:, e], ids[:, n], float(e), None, ALU.is_equal))
                    own.settle()
                    for e in range(E1):
                        last = own.add(pool.tensor_tensor(wm[:, e], wm[:, e], wts[:, n], ALU.mult))
                    own.restart()
                    pool.tensor_copy(wm_done[:], wm[0:1, 0, 0, 0:1]).then_inc(masked, 1)
                if finish:
                    pool.wait_ge(var_made, c)
                    pool.tensor_tensor(rstd[:], vare[:], k.minus_half[:, 0:TC, :], ALU.pow).then_inc(rstd_made, 1)
                    pool.wait_ge(x2_made, c)
                    pool.tensor_copy(X[:, bass.ds((c - 1) * TC, TC), :], x2s[:]).then_inc(x2_kept, 1)

            run_bodies(pool, body)
            pool.wait_ge(x2_kept, NCH + 1)

        @block.tensor
        def _(pe):
            pe.wait_ge(consts, 11)
            pe.wait_ge(loaded, 16)
            pe.wait_ge(w_lo, len(pieces))

            def body(c, par, scores, prepare, finish):
                nxt = prv = 1 - par

                def kept(name):
                    b, n = GATED.at(c, name)
                    pe.wait_ge(emptied[b], n)

                def item(name):
                    b, n = GATED.at(c, name)
                    bank = spare[b]
                    wait(pe, emptied[b], n - 1)
                    if name == "A sum":
                        pe.wait_ge(masked, c + 2)
                        for t in range(TC):
                            for e in range(E1):
                                col = 2 * t * E1 + e
                                last = pe.matmul(bank[0:L, col:col + E1 + 1:E1], wm[:, e, t], halves[:],
                                                 start=True, stop=True)
                    elif name == "A gT":
                        pe.wait_ge(gates_made, c + 2)
                        for b2 in range(BC):
                            last = pe.matmul(bank[0:3 * E1, L * b2:L * b2 + L],
                                             g3[:, b2].rearrange("p a e -> p (a e)"), identb[:, 0:L],
                                             start=True, stop=True)
                    elif name == "F oT":
                        pe.wait_ge(oT_kept, c)
                        for t in range(TC):
                            last = pe.transpose(bank[:, P * t:P * t + P], oT[:, P * t:P * t + P], ident[:])
                    elif name == "F xT":
                        pe.wait_ge(x2_made, c)
                        for t in range(TC):
                            last = pe.transpose(bank[:, P * t:P * t + P], x2s[:, t], ident[:])
                    elif name == "F rt":
                        kept("F xT")
                        for t in range(TC):
                            last = pe.matmul(bank[:, E2 * t:E2 * t + E2], x2T[:, P * t:P * t + P], Wr[:],
                                             start=True, stop=True)
                    elif name == "F cT":
                        pe.wait_ge(routed, c)
                        for t in range(TC):
                            last = pe.matmul(bank[0:3 * E2, P * t:P * t + P],
                                             cw3[:, t].rearrange("p a e -> p (a e)"), identb[:],
                                             start=True, stop=True)
                    last.then_inc(filled[b], 1)

                def project(u):
                    wait(pe, rectified, U1 * c + u - 1)
                    chunk = bass.ds(c * CW, CW)
                    bank = psH[u % 2]
                    pe.matmul(bank[:], Wih[:, u], XTh[:, chunk], start=True, stop=False)
                    pe.matmul(bank[:], Wih[:, u], XTl[:, chunk], start=False, stop=False)
                    pe.matmul(bank[:], Wil[:, u], XTh[:, chunk], start=False, stop=True).then_inc(hidden, 1)

                def spread_gate(u):
                    e = u // 2
                    if u == 0:
                        if isinstance(c, int) and c == 0:
                            b, n = GATED.at(-1, "A gT")
                            pe.wait_ge(emptied[b], n)
                    wait(pe, gated, U1 * c + u - 2)
                    pe.matmul(psG[e % 2][:], pick[:, e], GT[:, par], start=True, stop=True).then_inc(spread, 1)

                def add(u):
                    v, o = (u - LAG1) % U1, psO[par if u >= LAG1 else prv]
                    pe.wait_ge(lo_made, U1 * c + u - LAG1 + 1)
                    n = v % 4
                    pe.matmul(o[:], Woh[:, v], hh[:, n], start=(v == 0), stop=False)
                    pe.matmul(o[:], Wol[:, v], hh[:, n], start=False, stop=False)
                    pe.matmul(o[:], Woh[:, v], hl[:, n], start=False, stop=(v == U1 - 1)).then_inc(added, 1)

                for u in range(U1):
                    if scores:
                        project(u)
                        if u % 2 == 0:
                            spread_gate(u)
                    if (scores and u >= LAG1) or (u < LAG1 and finish):
                        add(u)
                    for name in GATED.now(u, prepare, finish):
                        item(name)

            run_bodies(pe, body)

        @block.scalar
        def _(act):
            for n, (w, i) in enumerate(pieces):
                act.wait_ge(staged[n % 4], 16 * (n // 4 + 1))
                act.copy((Wih, Woh)[w][:, PIECE * i:PIECE * (i + 1)], stage[:, n % 4]).then_inc(w_hi, 1)
            act.wait_ge(consts, 11)

            def body(c, par, scores, prepare, finish):
                nxt = prv = 1 - par

                def item(name):
                    if name in ("A sum", "F oT"):
                        return
                    b, n = GATED.at(c, name)
                    bank, chunk = spare[b], bass.ds((c - 1) * CW, CW)
                    if name == "F rt":
                        act.wait_ge(shifted, c)
                        act.activation(lg[:], lg[:], ACT.Exp).then_inc(raised, 1)
                        return
                    act.wait_ge(filled[b], n)
                    if name == "A gT":
                        act.copy(GT[:, nxt], bank[0:3 * E1]).then_inc(emptied[b], 1)
                    elif name == "F xT":
                        act.copy(x2T[:], bank[:]).then_inc(emptied[b], 1)
                        act.wait_ge(emptied[b], n)
                        act.copy(XTh[:, chunk], x2T[:]).then_inc(xh_kept, 1)
                    elif name == "F cT":
                        act.copy(CWT[0:3 * E2, chunk], bank[0:3 * E2]).then_inc(emptied[b], 1)

                def rectify(u):
                    act.wait_ge(hidden, U1 * c + u + 1)
                    wait(act, gated, U1 * c + u - 1)
                    act.activation(rr[:, u % 2], psH[u % 2][:], ACT.Relu).then_inc(rectified, 1)

                def high(u):
                    g = U1 * c + u - 1
                    act.wait_ge(gated, g + 1)
                    wait(act, added, g - 3)
                    act.copy(hh[:, (u - 1) % 4], hg[:, (u - 1) % 2]).then_inc(hi_made, 1)

                for u in range(U1):
                    if scores:
                        rectify(u)
                    if (scores and u >= 1) or (u == 0 and finish):
                        high(u)
                    if u == LAG1 and finish:
                        act.wait_ge(added, U1 * c)
                        act.copy(oT[:], psO[prv][:]).then_inc(oT_kept, 1)
                    for name in GATED.now(u, prepare, finish):
                        item(name)

            run_bodies(act, body)

        @block.vector
        def _(dve):
            own = Own(dve, own_v)
            tt, ts, stt = dve.tensor_tensor, dve.tensor_scalar, dve.scalar_tensor_tensor
            for n, (w, i) in enumerate(pieces):
                tiles = slice(PIECE * i, PIECE * (i + 1))
                dve.wait_ge(w_hi, n + 1)
                tt((Wil, Wol)[w][:, tiles], stage[:, n % 4], (Wih, Woh)[w][:, tiles].bitcast(F32), ALU.subtract
                   ).then_inc(w_lo, 1)
            dve.wait_ge(consts, 11)

            def body(c, par, scores, prepare, finish):
                nxt = prv = 1 - par

                def took(name):
                    b, n = GATED.at(c, name)
                    dve.wait_ge(filled[b], n)
                    return spare[b], emptied[b]

                def gate(u):
                    g = U1 * c + u
                    if u % 2 == 0:
                        dve.wait_ge(spread, U1 // 2 * c + u // 2 + 1)
                    wait(dve, hi_made, g - 1)
                    wait(dve, lo_made, g - 1)
                    dve.wait_ge(rectified, g + 1)
                    tt(hg[:, u % 2], rr[:, u % 2], psG[u // 2 % 2][:], ALU.mult).then_inc(gated, 1)

                def low(u):
                    g, n = U1 * c + u - 1, (u - 1) % 4
                    wait(dve, added, g - 3)
                    dve.wait_ge(hi_made, g + 1)
                    tt(hl[:, n], hg[:, (u - 1) % 2], hh[:, n].bitcast(F32), ALU.subtract).then_inc(lo_made, 1)

                def split_gates():
                    bank, done = took("A sum")
                    s = bank[0:L, 0:BC * E1].rearrange("p (b e) -> p b e", e=E1)
                    own.add(dve.tensor_copy(g3[0:L, :, 0], s))
                    own.settle()
                    tt(gr[:], s, g3[0:L, :, 0], ALU.subtract).then_inc(done, 1)
                    b, n = GATED.at(c, "A sum")
                    dve.wait_ge(emptied[b], n)
                    own.add(dve.tensor_copy(g3[0:L, :, 1], gr[:]))
                    own.settle()
                    tt(g3[0:L, :, 2], gr[:], g3[0:L, :, 1], ALU.subtract).then_inc(gates_made, 1)

                def residual():
                    bank, done = took("F oT")
                    tt(y[:], bank[:].rearrange("p (t d) -> p t d", t=TC), X[:, bass.ds((c - 1) * TC, TC), :],
                       ALU.add).then_inc(done, 1)
                    b, n = GATED.at(c, "F oT")
                    dve.wait_ge(emptied[b], n)
                    for t in range(TC):
                        own.add(dve.bn_stats(stats[:, t], y[:, t]))
                    own.settle()
                    for t in range(TC):
                        own.add(dve.bn_aggr(mv[:, t], stats[:, t]))
                    own.settle()
                    ts(vare[:], mv[:, :, 1:2], EPS, None, ALU.add).then_inc(var_made, 1)

                def normalize():
                    dve.wait_ge(rstd_made, c)
                    dve.wait_ge(x2_kept, c)
                    for t in range(TC):
                        last = ts(x2s[:, t], y[:, t], mv[:, t, 0:1], rstd[:, t], ALU.subtract, ALU.mult)
                    last.then_inc(x2_made, 1)

                def keep_low():
                    chunk = bass.ds((c - 1) * CW, CW)
                    dve.wait_ge(xh_kept, c)
                    own.add(tt(XTl[:, chunk], x2T[:], XTh[:, chunk].bitcast(F32), ALU.subtract))

                def shift():
                    bank, done = took("F rt")
                    s = bank[:, 0:TC * E2].rearrange("p (t e) -> p t e", e=E2)
                    own.add(dve.tensor_reduce(lmax[:, :, 0], s, X_AXIS, ALU.max, negate=True))
                    own.settle()
                    tt(lg[:], s, lmax[:].to_broadcast([P, TC, E2]), ALU.add).then_inc(shifted, 1)
                    dve.tensor_copy(freeing[:], bank[0:1, 0:1]).then_inc(done, 1)

                def route():
                    dve.wait_ge(raised, c)
                    own.add(dve.reduce_sum(lsum[:], lg[:], axis=X_AXIS))
                    own.settle()
                    own.add(dve.reciprocal(lrec[:, :, 0], lsum[:]))
                    own.settle()
                    own.add(tt(pr0[:, :, 0:E2], lg[:], lrec[:].to_broadcast([P, TC, E2]), ALU.mult))
                    own.settle()
                    for t in range(TC):
                        own.add(dve.max(mx8[:, t], pr0[:, t]))
                    own.settle()
                    for t in range(TC):
                        own.add(dve.match_replace(pr1[:, t], mx8[:, t], pr0[:, t], -BIG))
                    own.settle()
                    own.add(stt(cw[:], pr1[:, :, 0:E2], -BIG, pr0[:, :, 0:E2], ALU.is_le, ALU.mult))
                    own.settle()
                    own.add(dve.tensor_copy(cw3[:, :, 0], cw[:]))
                    own.settle()
                    own.add(tt(cwr[:], cw[:], cw3[:, :, 0], ALU.subtract))
                    own.settle()
                    own.add(dve.tensor_copy(cw3[:, :, 1], cwr[:]))
                    own.settle()
                    tt(cw3[:, :, 2], cwr[:], cw3[:, :, 1], ALU.subtract).then_inc(routed, 1)

                for u in range(U1):
                    if scores:
                        gate(u)
                    if (scores and u >= 1) or (u == 0 and finish):
                        low(u)
                    if u == 4 and finish:
                        residual()
                    if u == 6 and finish:
                        normalize()
                    if u == 9 and finish:
                        keep_low()
                    if u == 10 and prepare:
                        split_gates()
                    if u == 11 and finish:
                        shift()
                    if u == 12 and finish:
                        route()
                if own.n:
                    own.restart()

            run_bodies(dve, body)


U2 = E2 * F2 // P + 1
LAG2 = 2


def routed_experts(nc, k, w_gate, w_up, w_down, out):
    with ExitStack() as ctx:
        def sb(name, shape, dt=F32):
            return ctx.enter_context(nc.sbuf_tensor(name, shape, dt))

        def ps(name, shape, dt=F32):
            return ctx.enter_context(nc.psum_tensor(name, shape, dt))

        def sem(name):
            return ctx.enter_context(nc.semaphore(name))

        X, XTh, XTl, ident, CWT = k.X, k.XTh, k.XTl, k.ident, k.CWT
        stage = sb("stage3", [P, 3, 3, P])
        parts = {}
        for name in ("gate", "up", "down"):
            parts[name] = (sb(f"W{name}h", [P, U2, P], F32R), sb(f"W{name}l", [P, U2, P], F32R))
        pick = sb("pick3", [P, U2 - 1, 2, F2], BF16)
        sg, tu, hg = sb("sg", [P, 2, CW]), sb("tu", [P, 2, CW]), sb("hg3", [P, 2, CW])
        hh, hl = sb("hh3", [P, 3, CW], F32R), sb("hl3", [P, 3, CW], F32R)
        oT = sb("oT3", [P, CW])
        y, x3s = sb("y3", [P, TC, D]), sb("x3s", [P, 2, TC, D])
        stats, mv = sb("stats3", [P, TC, 6]), sb("mv3", [P, TC, 2])
        vare, rstd = sb("vare3", [P, TC, 1]), sb("rstd3", [P, TC, 1])

        psg = [ps(f"psgate{i}", [P, 512]) for i in range(2)]
        psu = [ps(f"psup{i}", [P, 512]) for i in range(2)]
        psc = ps("psweight", [P, 512])
        psO = [ps(f"psdown{i}", [P, 512]) for i in range(2)]
        psT = ps("psturn", [P, 512])

        staged = [sem(f"experts_staged{i}") for i in range(3)]
        w_hi, w_lo = sem("experts_high_made"), sem("experts_low_made")
        consts = sem("constants_made3")
        own_v = sem("vector_results3")
        gate_up = sem("gate_and_up_filled")
        weight = sem("weight_spread")
        silu_made = sem("silu_made")
        gated = sem("hidden_weighed")
        hi_made, lo_made = sem("hidden_high_made3"), sem("hidden_low_made3")
        added = sem("unit_added3")
        oT_kept = sem("output_in_sbuf3")
        turned = sem("output_turned")
        y_made = sem("residual_made3")
        var_made, rstd_made = sem("variance_made3"), sem("rstd_made3")
        x3_made = sem("x3_made")
        stored = [sem(f"x3_stored{i}") for i in range(2)]

        block = ctx.enter_context(nc.Block())
        pieces = [(name, i) for i in range(U2 // 3) for name in ("gate", "up", "down")]
        sources = {"gate": w_gate, "up": w_up, "down": w_down}

        def run(engine, body):
            body(0, 0, scores=True, finish=False)
            with engine.Fori(0, (NCH - 2) // 2) as pair:
                body(2 * pair + 1, 1, scores=True, finish=True)
                body(2 * pair + 2, 0, scores=True, finish=True)
            body(NCH - 1, 1, scores=True, finish=True)
            body(NCH, 0, scores=False, finish=True)

        @block.sync
        def _(sp):
            for n, (name, i) in enumerate(pieces):
                if n >= 3:
                    sp.wait_ge(w_lo, n - 2)
                sp.dma_start(stage[:, n % 3], sources[name][:, 3 * i:3 * i + 3, :]).then_inc(staged[n % 3], 16)

            def body(c, par, scores, finish):
                if finish:
                    prv = 1 - par
                    sp.wait_ge(x3_made, c)
                    dst = out[bass.ds(BC * (c - 1), BC)].rearrange("(t b) l d -> b l t d", b=2)
                    for b2 in range(2):
                        sp.dma_start(dst[b2], x3s[L * b2:L * b2 + L, prv]).then_inc(stored[prv], 16)

            run(sp, body)
            for par in range(2):
                sp.wait_ge(stored[par], 32 * (NCH // 2 + 1))

        @block.gpsimd
        def _(pool):
            for par in range(2):
                pool.memset(x3s[:, par], 0.0).then_inc(stored[par], 32)
            pool.memset(pick[:], 0.0).then_inc(consts, 1)
            pool.wait_ge(consts, 1)
            for part in range(3):
                pool.affine_select(out=pick[:], in_=pick[:], compare_op=ALU.not_equal, fill=1.0, base=-E2 * part,
                                   pattern=[[-2, U2 - 1], [-1, 2], [0, F2]], channel_multiplier=1).then_inc(consts, 1)
                pool.wait_ge(consts, 2 + part)

            def body(c, par, scores, finish):
                if finish:
                    pool.wait_ge(var_made, c)
                    pool.tensor_tensor(rstd[:], vare[:], k.minus_half[:, 0:TC, :], ALU.pow).then_inc(rstd_made, 1)

            run(pool, body)
            pool.wait_ge(rstd_made, NCH)

        @block.tensor
        def _(pe):
            pe.wait_ge(consts, 4)
            pe.wait_ge(w_lo, len(pieces))

            def body(c, par, scores, finish):
                prv = 1 - par

                def three(bank, w, j, hi, lo, start, stop):
                    wh, wl = parts[w]
                    pe.matmul(bank, wh[:, j], hi, start=start, stop=False)
                    pe.matmul(bank, wl[:, j], hi, start=False, stop=False)
                    return pe.matmul(bank, wh[:, j], lo, start=False, stop=stop)

                def project(j):
                    g, b = U2 * c + j, (par + j) % 2
                    chunk = bass.ds(c * CW, CW)
                    wait(pe, silu_made, g - 1)
                    three(psg[b][:], "gate", j, XTh[:, chunk], XTl[:, chunk], True, True)
                    wait(pe, gated, g - 1)
                    three(psu[b][:], "up", j, XTh[:, chunk], XTl[:, chunk], True, True).then_inc(gate_up, 1)

                def spread(j):
                    wait(pe, gated, U2 * c + j)
                    pe.matmul(psc[:], pick[:, j].rearrange("p a f -> p (a f)"), CWT[:, bass.ds(c * CW, CW)],
                              start=True, stop=True).then_inc(weight, 1)

                def add(j):
                    v, o = (j - LAG2) % U2, psO[par if j >= LAG2 else prv]
                    n = v % 3
                    pe.wait_ge(lo_made, U2 * c + j - LAG2 + 1)
                    three(o[:], "down", v, hh[:, n], hl[:, n], v == 0, v == U2 - 1).then_inc(added, 1)

                for j in range(U2):
                    if scores:
                        project(j)
                    if (scores and j >= LAG2) or (j < LAG2 and finish):
                        add(j)
                    if scores and j < U2 - 1:
                        spread(j)
                    if j == LAG2 + 1 and finish:
                        pe.wait_ge(oT_kept, c)
                        for t in range(TC):
                            last = pe.transpose(psT[:, P * t:P * t + P], oT[:, P * t:P * t + P], ident[:])
                        last.then_inc(turned, 1)

            run(pe, body)

        @block.scalar
        def _(act):
            for n, (name, i) in enumerate(pieces):
                act.wait_ge(staged[n % 3], 16 * (n // 3 + 1))
                act.copy(parts[name][0][:, 3 * i:3 * i + 3], stage[:, n % 3]).then_inc(w_hi, 1)

            def body(c, par, scores, finish):
                prv = 1 - par

                def silu(j):
                    g, b = U2 * c + j, (par + j) % 2
                    act.wait_ge(gate_up, g + 1)
                    wait(act, gated, g - 1)
                    act.activation(sg[:, b], psg[b][:], ACT.Silu).then_inc(silu_made, 1)

                def high(j):
                    g = U2 * c + j - 1
                    act.wait_ge(gated, g + 1)
                    wait(act, added, g - 2)
                    act.copy(hh[:, (j - 1) % 3], hg[:, (par + j - 1) % 2]).then_inc(hi_made, 1)

                for j in range(U2):
                    if scores:
                        silu(j)
                    if (scores and j >= 1) or (j == 0 and finish):
                        high(j)
                    if j == LAG2 and finish:
                        act.wait_ge(added, U2 * c)
                        act.copy(oT[:], psO[prv][:]).then_inc(oT_kept, 1)

            run(act, body)

        @block.vector
        def _(dve):
            own = Own(dve, own_v)
            tt, ts = dve.tensor_tensor, dve.tensor_scalar
            for n, (name, i) in enumerate(pieces):
                dve.wait_ge(w_hi, n + 1)
                wh, wl = parts[name]
                tt(wl[:, 3 * i:3 * i + 3], stage[:, n % 3], wh[:, 3 * i:3 * i + 3].bitcast(F32), ALU.subtract
                   ).then_inc(w_lo, 1)

            def body(c, par, scores, finish):
                prv = 1 - par

                def weigh(j):
                    g, b = U2 * c + j, (par + j) % 2
                    dve.wait_ge(silu_made, g + 1)
                    wait(dve, hi_made, g - 1)
                    wait(dve, lo_made, g - 1)
                    if j == U2 - 1:
                        tt(hg[:, b], sg[:, b], psu[b][:], ALU.mult).then_inc(gated, 1)
                    else:
                        own.add(tt(tu[:, b], sg[:, b], psu[b][:], ALU.mult))
                        own.settle()
                        dve.wait_ge(weight, (U2 - 1) * c + j + 1)
                        tt(hg[:, b], tu[:, b], psc[:], ALU.mult).then_inc(gated, 1)

                def low(j):
                    g, n = U2 * c + j - 1, (j - 1) % 3
                    wait(dve, added, g - 2)
                    dve.wait_ge(hi_made, g + 1)
                    tt(hl[:, n], hg[:, (par + j - 1) % 2], hh[:, n].bitcast(F32), ALU.subtract).then_inc(lo_made, 1)

                def residual():
                    dve.wait_ge(turned, c)
                    tt(y[:], psT[:].rearrange("p (t d) -> p t d", t=TC), X[:, bass.ds((c - 1) * TC, TC), :],
                       ALU.add).then_inc(y_made, 1)
                    dve.wait_ge(y_made, c)
                    for t in range(TC):
                        own.add(dve.bn_stats(stats[:, t], y[:, t]))
                    own.settle()
                    for t in range(TC):
                        own.add(dve.bn_aggr(mv[:, t], stats[:, t]))
                    own.settle()
                    ts(vare[:], mv[:, :, 1:2], EPS, None, ALU.add).then_inc(var_made, 1)

                def normalize():
                    dve.wait_ge(rstd_made, c)
                    dve.wait_ge(stored[prv], 16 * (c - 1 - prv) + 32)
                    for t in range(TC):
                        last = ts(x3s[:, prv, t], y[:, t], mv[:, t, 0:1], rstd[:, t], ALU.subtract, ALU.mult)
                    last.then_inc(x3_made, 1)

                for j in range(U2):
                    if scores:
                        weigh(j)
                    if (scores and j >= 1) or (j == 0 and finish):
                        low(j)
                    if j == 4 and finish:
                        residual()
                    if j == 6 and finish:
                        normalize()
                if own.n:
                    own.restart()

            run(dve, body)


class Kept:
    pass


def setup(nc, ctx):
    k = Kept()
    k.X = ctx.enter_context(nc.sbuf_tensor("X", [P, NCH * TC, D], F32))
    k.XTh = ctx.enter_context(nc.sbuf_tensor("XTh", [P, NCH * CW], F32R))
    k.XTl = ctx.enter_context(nc.sbuf_tensor("XTl", [P, NCH * CW], F32R))
    k.ident = ctx.enter_context(nc.sbuf_tensor("ident", [P, P], F32))
    k.minus_half = ctx.enter_context(nc.sbuf_tensor("minus_half", [P, TC, 1], F32))
    made = ctx.enter_context(nc.semaphore("identity_made"))
    with nc.Block() as block:
        @block.gpsimd
        def _(pool):
            pool.memset(k.minus_half[:], -0.5).then_inc(made, 1)
            pool.memset(k.ident[:], 0.0).then_inc(made, 1)
            pool.wait_ge(made, 2)
            pool.affine_select(out=k.ident[:], in_=k.ident[:], compare_op=ALU.not_equal, fill=1.0, base=0,
                               pattern=[[-1, P]], channel_multiplier=1).then_inc(made, 1)
            pool.wait_ge(made, 3)
    return k


def program(nc, a, out):
    with ExitStack() as ctx:
        k = setup(nc, ctx)
        attention(nc, k, a["x"], a["L0_attn_Wq"], a["L0_attn_bq"], a["L0_attn_Wk"], a["L0_attn_bk"],
                  a["L0_attn_Wv"], a["L0_attn_bv"], a["L0_attn_Wo"], a["L0_attn_bo"], a["L0_attn_sample_idx"])
        k.CWT = ctx.enter_context(nc.sbuf_tensor("CWT", [P, NCH * CW], BF16))
        gated_experts(nc, k, a["ctx_512"], a["itok_BxS2xS_0_7"], a["w_in"], a["w_out"], a["L0_ffn_Wr"])
        routed_experts(nc, k, a["w_gate"], a["w_up"], a["w_down"], out)


def kernel(**inputs):
    import numpy as np
    import concourse.bacc as bacc
    from concourse.bass_utils import run_bass_kernel_spmd as run

    v = {name: np.asarray(value) for name, value in inputs.items()}
    v["w_in"] = v.pop("L0_xattn_proj_in").transpose(2, 0, 1).reshape(D, U1, P)
    v["w_out"] = v.pop("L0_xattn_proj_out").reshape(E1, D, HID1 // P, P).transpose(3, 0, 2, 1).reshape(P, U1, D)
    for name, routed, shared in (("w_gate", "Wg", "Sg"), ("w_up", "Wu", "Su")):
        tiles = v.pop("L0_ffn_" + routed).transpose(1, 0, 2).reshape(D, U2 - 1, P)
        v[name] = np.concatenate([tiles, v.pop("L0_ffn_" + shared).reshape(D, 1, P)], axis=1)
    tiles = v.pop("L0_ffn_Wd").reshape(U2 - 1, P, D).transpose(1, 0, 2)
    v["w_down"] = np.concatenate([tiles, v.pop("L0_ffn_Sd").reshape(P, 1, D)], axis=1)

    nc = bacc.Bacc("TRN2", target_bir_lowering=False, num_devices=1)
    arrays, aps = {}, {}
    for name, value in v.items():
        arrays["in_" + name] = np.ascontiguousarray(value)
        aps[name] = nc.dram_tensor("in_" + name, value.shape, mybir.dt.from_np(value.dtype),
                                   kind="ExternalInput").ap()
    out = nc.dram_tensor("out", (B, L, D), F32, kind="ExternalOutput").ap()
    program(nc, aps, out)
    return run(nc, [arrays], core_ids=[0]).results[0]["out"]
```

```python
from contextlib import ExitStack

import concourse.bass as bass
from concourse import mybir

F32 = mybir.dt.float32
F32R = mybir.dt.float32r
F16 = mybir.dt.float16
BF16 = mybir.dt.bfloat16
I32 = mybir.dt.int32
U32 = mybir.dt.uint32
ALU = mybir.AluOpType
ACT = mybir.ActivationFunctionType
X_AXIS = mybir.AxisListType.X

P = 128
B = 128
L = 64
D = 128
H = 16
HD = D // H
NS = 35
NTOP = 25
TC = 4
BC = 2 * TC
CW = TC * P
NCH = B // BC
UNITS = 2 * TC
KW = L + NS + 2
SW = L + NS + 1
SCALE = float(HD) ** -0.5
BIG = 3.0e38
EPS = 1e-5


def wait(engine, semaphore, value):
    if isinstance(value, int) and value <= 0:
        return
    engine.wait_ge(semaphore, value)


class Own:

    def __init__(self, engine, semaphore):
        self.engine, self.semaphore, self.n = engine, semaphore, 0

    def add(self, instruction):
        self.n += 1
        return instruction.then_inc(self.semaphore, 1)

    def settle(self):
        self.engine.wait_ge(self.semaphore, self.n)

    def restart(self):
        self.settle()
        self.engine.sem_clear(self.semaphore)
        self.n = 0


SLOTS = [
    ["A xT", "F mT", "A xS"],
    ["A q", "A k0"],
    ["A v", "A k1"],
    ["A sq0", "A sq1", "F sel"],
    ["A sq2", "A sq3", "A sk00", "A sk01"],
    ["F aT", "A sk10", "F y", "A sk11"],
    ["A sk20", "A sk21", "A sk30"],
    ["A vm", "A sk31", "F x1T"],
]


class Plan:

    def __init__(self, slots):
        self.slots = slots
        every = [n for s in slots for n in s]
        self.items = {"A": [n for n in every if n[0] == "A"], "F": [n for n in every if n[0] == "F"], "AF": every}
        assert len(every) % 2 == 0

    def at(self, c, name):
        a, f, af = (self.items[i] for i in ("A", "F", "AF"))
        if isinstance(c, int) and c <= 0:
            n = (c + 1) * len(a) + a.index(name)
            return n % 2, n // 2 + 1
        if isinstance(c, int) and c >= NCH - 1:
            n = 2 * len(a) + len(af) * (NCH - 2) + (c - NCH + 1) * len(f) + f.index(name)
            return n % 2, n // 2 + 1
        n = af.index(name)
        return n % 2, (c - 1) * (len(af) // 2) + len(a) + n // 2 + 1

    def now(self, u, prepare, finish):
        return [n for n in self.slots[u] if (prepare if n[0] == "A" else finish)]


ATTENTION = Plan(SLOTS)
spare_bank = ATTENTION.at


def loads_of(c, par):
    return 16 * c + 32 - 16 * par


def run_bodies(engine, body):
    body(-1, 1, scores=False, prepare=True, finish=False)
    body(0, 0, scores=True, prepare=True, finish=False)
    with engine.Fori(0, (NCH - 2) // 2) as pair:
        body(2 * pair + 1, 1, scores=True, prepare=True, finish=True)
        body(2 * pair + 2, 0, scores=True, prepare=True, finish=True)
    body(NCH - 1, 1, scores=True, prepare=False, finish=True)
    body(NCH, 0, scores=False, prepare=False, finish=True)


def attention(nc, k, x, wq, bq, wk, bk, wv, bv, wo, bo, sample_idx):
    with ExitStack() as ctx:
        def sb(name, shape, dt=F32):
            return ctx.enter_context(nc.sbuf_tensor(name, shape, dt))

        def ps(name, shape, dt=F32):
            return ctx.enter_context(nc.psum_tensor(name, shape, dt))

        def sem(name):
            return ctx.enter_context(nc.semaphore(name))

        X, XTh, XTl, ident = k.X, k.XTh, k.XTl, k.ident

        Wq, Wk, Wv, Wo = (sb(n, [P, D]) for n in ("Wq", "Wk", "Wv", "Wo"))
        Wqs = sb("Wqs", [P, D])
        bqc, bkc, bqs = sb("bqc", [P, 1]), sb("bkc", [P, 1]), sb("bqs", [P, 1])
        bvc = sb("bvc", [P, 1])
        bof = sb("bof", [P, D])
        idx = sb("idx", [P, NS], I32)
        idf, neg = sb("idf", [P, NS]), sb("neg", [P, NS])
        lrow = sb("lrow", [P, 1], I32)
        lrowf = sb("lrowf", [P, 1])
        hot, cnt = sb("hot", [P, NS]), sb("cnt", [P, 1])
        SELW = NS + 2
        selbd = sb("selbd", [P, 2, SELW])
        rep = sb("rep", [P, 4, 4, P], F16)
        xin = sb("xin", [P, 2, TC, D])
        xb = sb("xb", [P, 2, TC, D])
        xT = sb("xT", [P, BC, KW])
        qhi, qlo = sb("qhi", [P, BC, L], F16), sb("qlo", [P, BC, L], F16)
        khi, klo = sb("khi", [P, BC, KW], F16), sb("klo", [P, BC, KW], F16)
        QS = sb("QS", [P, 2, 4, BC, L], F16)
        KS = sb("KS", [P, 2, 4, BC, SW], F16)
        VB = sb("VB", [P, 2, BC, H // 2, 2 * (HD + 1)])
        att = sb("att", [P, 2, TC, D])
        nmax, smax = sb("nmax", [P, 2, 8]), sb("smax", [P, 2, 8])
        PR = sb("PR", [P, 2, 8, L])
        PT = sb("PT", [P, 2, 4, P])
        M = sb("M", [P, 2, TC * H])
        ROUNDS = (NTOP + 7) // 8
        NSENT = 8 * ROUNDS - NTOP
        top0, top1 = sb("top0", [P, L + NSENT]), sb("top1", [P, L + NSENT])
        mx8 = sb("mx8", [P, 8])
        freeing = sb("freeing", [1, 1])
        chosen = sb("chosen", [P, L])
        selT = sb("selT", [P, TC * H])
        O9 = sb("O9", [P, 2, TC, H, HD + 1])
        rden = sb("rden", [P, TC, H])
        onorm = sb("onorm", [P, TC, H, HD])
        attT = sb("attT", [P, CW])
        y = sb("y", [P, TC, D])
        stats, mv = sb("stats", [P, TC, 6]), sb("mv", [P, TC, 2])
        vare, rstd = sb("vare", [P, TC, 1]), sb("rstd", [P, TC, 1])
        nmean, shift = sb("nmean", [P, TC, 1]), sb("shift", [P, TC, 1])
        x1s, x1T = sb("x1s", [P, TC, D]), sb("x1T", [P, CW])

        psS = [ps(f"psS{i}", [P, 2, 512]) for i in range(2)]
        psP = ps("psP", [P, 4, P])
        psO = ps("psO", [P, H * (HD + 1)])
        spare = [ps(f"spare{i}", [P, 512]) for i in range(2)]

        loaded = sem("weights_loaded")
        consts = sem("constants_made")
        folded = sem("constants_folded")
        bias_through = sem("value_bias_through_output_weights")
        x_loaded = [sem(f"x_loaded{i}") for i in range(2)]
        xb_made = sem("x_plus_bias_made")
        filled = [sem(f"spare{i}_filled") for i in range(2)]
        emptied = [sem(f"spare{i}_emptied") for i in range(2)]
        hi_made = sem("high_parts_made")
        scored = sem("scores_filled")
        scores_read = sem("scores_read")
        shifted = sem("scores_shifted")
        probs = sem("probabilities_made")
        turned = sem("probabilities_turned")
        turned_kept = sem("turned_probabilities_in_sbuf")
        weighed = sem("values_weighed")
        out_read = sem("output_tile_read")
        chosen_made = sem("choice_made")
        mixed = sem("heads_mixed")
        var_made = sem("variance_made")
        rstd_made = sem("rstd_made")
        x1_made = sem("x1_made")
        x1_kept = sem("x1_kept")
        shift_made = sem("shift_made")
        hi_kept, lo_kept = sem("x1_high_part_kept"), sem("x1_low_part_kept")
        own_v = sem("vector_results")

        FOLDED = 9

        block = ctx.enter_context(nc.Block())

        @block.sync
        def _(sp):
            for dst, src in ((Wq, wq), (Wk, wk), (Wv, wv), (Wo, wo)):
                sp.dma_start(dst[:], src).then_inc(loaded, 16)
            sp.dma_start(bqc[:], bq.rearrange("(e a) -> e a", a=1)).then_inc(loaded, 16)
            sp.dma_start(bkc[:], bk.rearrange("(e a) -> e a", a=1)).then_inc(loaded, 16)
            sp.dma_start(bvc[:], bv.rearrange("(e a) -> e a", a=1)).then_inc(loaded, 16)
            sp.dma_start(bof[:], bo.partition_broadcast(P)).then_inc(loaded, 16)
            sp.dma_start(idx[:], sample_idx.partition_broadcast(P)).then_inc(loaded, 16)

            def load(c, par):
                for b2 in range(2):
                    src = x[bass.ds(BC * c, BC)].rearrange("(t b) l d -> b l t d", b=2)
                    sp.dma_start(xin[L * b2:L * b2 + L, par], src[b2]).then_inc(x_loaded[par], 16)

            load(0, 0)
            load(1, 1)
            with sp.Fori(0, (NCH - 2) // 2) as pair:
                sp.wait_ge(xb_made, 2 * pair + 1)
                load(2 * pair + 2, 0)
                sp.wait_ge(xb_made, 2 * pair + 2)
                load(2 * pair + 3, 1)

        @block.gpsimd
        def _(pool):
            pool.iota(lrow[0:L], pattern=[[0, 1]], base=0, channel_multiplier=1).then_inc(consts, 1)
            pool.wait_ge(consts, 1)
            pool.iota(lrow[L:P], pattern=[[0, 1]], base=0, channel_multiplier=1).then_inc(consts, 1)
            pool.wait_ge(consts, 2)
            pool.memset(rep[:], 0.0).then_inc(consts, 1)
            pool.memset(selbd[:], 0.0).then_inc(consts, 1)
            pool.memset(VB[:], 0.0).then_inc(consts, 1)
            pool.memset(top0[:], BIG).then_inc(consts, 1)
            pool.memset(rstd[:], 0.0).then_inc(x1_kept, 1)
            pool.wait_ge(consts, 6)
            for half in range(2):
                pool.memset(VB[L * half:L * half + L, :, :, :, (HD + 1) * half + HD], 1.0).then_inc(consts, 1)
                pool.wait_ge(consts, 7 + half)
            for kind, (k0, k1) in enumerate(((0, 1), (2, 3), (0, 2), (1, 3))):
                for t in range(4):
                    v = rep[:, kind, t].rearrange("p (j k d) -> p j k d", j=4, k=4)[:, :, k0:k1 + 1:k1 - k0, :]
                    pool.affine_select(out=v, in_=v, compare_op=ALU.not_equal, fill=1.0, base=-HD * t,
                                       pattern=[[-32, 4], [0, 2], [-1, HD]], channel_multiplier=1
                                       ).then_inc(consts, 1)

            def body(c, par, scores, prepare, finish):
                n = 1 - par
                if finish:
                    pool.wait_ge(var_made, 2 * c)
                    pool.tensor_tensor(rstd[:], vare[:], k.minus_half[:, 0:TC, :], ALU.pow).then_inc(rstd_made, 1)
                    pool.wait_ge(rstd_made, c)
                    pool.tensor_tensor(shift[:], nmean[:], rstd[:], ALU.mult).then_inc(shift_made, 1)
                    pool.wait_ge(x1_made, c)
                    pool.tensor_copy(X[:, bass.ds((c - 1) * TC, TC), :], x1s[:]).then_inc(x1_kept, 1)
                    pool.wait_ge(hi_kept, c)
                    chunk = bass.ds((c - 1) * CW, CW)
                    pool.tensor_tensor(XTl[:, chunk], x1T[:], XTh[:, chunk].bitcast(F32), ALU.subtract
                                       ).then_inc(lo_kept, 1)
                if prepare:
                    pool.wait_ge(x_loaded[n], loads_of(c + 1, n))
                    b, m = spare_bank(c, "A xS")
                    pool.wait_ge(emptied[b], m)
                    bias = bof[:].rearrange("p (a d) -> p a d", a=1).to_broadcast([P, TC, D])
                    pool.tensor_tensor(xb[:, n], xin[:, n], bias, ALU.add).then_inc(xb_made, 1)

            pool.wait_ge(folded, FOLDED)
            run_bodies(pool, body)
            pool.wait_ge(x1_kept, NCH + 1)
            pool.wait_ge(lo_kept, NCH)

        @block.tensor
        def _(pe):
            pe.wait_ge(loaded, 16 * 9)
            pe.matmul(psO[:, 0:D], bvc[:].to_broadcast([P, P]), Wo[:], start=True, stop=True
                      ).then_inc(bias_through, 1)
            pe.wait_ge(consts, 24)
            pe.wait_ge(folded, FOLDED)

            def body(c, par, scores, prepare, finish):
                nxt = prv = 1 - par

                def item(name):
                    b, n = spare_bank(c, name)
                    bank = spare[b]
                    wait(pe, emptied[b], n - 1)

                    def kept(earlier):
                        b2, n2 = spare_bank(c, earlier)
                        if b2 != b:
                            pe.wait_ge(emptied[b2], n2)

                    if name == "A xT":
                        pe.wait_ge(x_loaded[nxt], loads_of(c + 1, nxt))
                        for t in range(TC):
                            last = pe.transpose(bank[:, P * t:P * t + P], xin[:, nxt, t], ident[:])
                    elif name == "A xS":
                        for t in range(TC):
                            last = pe.matmul(bank[:, 2 * SELW * t:2 * SELW * (t + 1)], xin[:, nxt, t],
                                             selbd[:].rearrange("p b s -> p (b s)"), start=True, stop=True)
                    elif name == "A q":
                        kept("A xT")
                        kept("A xS")
                        last = pe.matmul(bank[:], Wqs[:], xT[:, :, 0:L], start=True, stop=True)
                    elif name in ("A k0", "A k1"):
                        h = int(name[-1])
                        last = pe.matmul(bank[:, 0:4 * KW], Wk[:],
                                         xT[:, 4 * h:4 * h + 4, :].rearrange("p b s -> p (b s)"),
                                         start=True, stop=True)
                    elif name == "A v":
                        wvh = Wv[:].rearrange("p (a b d) -> p a b d", b=2, d=HD)
                        for n in range(BC):
                            for hh in range(2):
                                last = pe.matmul(bank[L * hh:L * hh + L, L * n:L * n + L], xT[:, n, 0:L],
                                                 wvh[:, :, hh, :], start=True, stop=True)
                    elif name == "A vm":
                        for n in range(BC):
                            mean = xT[:, n, KW - 1:KW].to_broadcast([P, L])
                            last = pe.matmul(bank[L * (n % 2):L * (n % 2) + L, P * (n // 2):P * (n // 2) + P],
                                             mean, Wv[:], start=True, stop=True)
                    elif name[:4] == "A sq":
                        t = int(name[4])
                        kept("A q")
                        pe.matmul(bank[:], rep[:, 0, t], qhi[:].rearrange("p b l -> p (b l)"), start=True, stop=False)
                        last = pe.matmul(bank[:], rep[:, 1, t], qlo[:].rearrange("p b l -> p (b l)"),
                                         start=False, stop=True)
                    elif name[:4] == "A sk":
                        t, h = int(name[4]), int(name[5])
                        kept("A k1")
                        pe.matmul(bank[:, 0:4 * SW], rep[:, 2, t], khi[:, 4 * h:4 * h + 4, 0:SW],
                                  start=True, stop=False)
                        last = pe.matmul(bank[:, 0:4 * SW], rep[:, 3, t], klo[:, 4 * h:4 * h + 4, 0:SW],
                                         start=False, stop=True)
                    elif name == "F mT":
                        pe.wait_ge(scores_read, UNITS * c)
                        last = pe.matmul(bank[0:TC * H, 0:P], M[:, prv], ident[:], start=True, stop=True)
                    elif name == "F sel":
                        pe.wait_ge(chosen_made, c)
                        last = pe.matmul(bank[0:L, 0:P], chosen[:], ident[:], start=True, stop=True)
                    elif name == "F aT":
                        pe.wait_ge(mixed, c)
                        for t in range(TC):
                            last = pe.transpose(bank[:, P * t:P * t + P], att[:, prv, t], ident[:])
                    elif name == "F y":
                        kept("F aT")
                        for t in range(TC):
                            last = pe.matmul(bank[:, P * t:P * t + P], attT[:, P * t:P * t + P], Wo[:],
                                             start=True, stop=True)
                    elif name == "F x1T":
                        pe.wait_ge(x1_made, c)
                        for t in range(TC):
                            last = pe.transpose(bank[:, P * t:P * t + P], x1s[:, t], ident[:])
                    last.then_inc(filled[b], 1)

                def score(u):
                    t, jp = u // 2, u % 2
                    if u == 0:
                        if isinstance(c, int) and c == 0:
                            for name in ("A sk30", "A sk31"):
                                b, n = spare_bank(-1, name)
                                pe.wait_ge(emptied[b], n)
                        else:
                            pe.wait_ge(probs, UNITS * c)
                    wait(pe, scores_read, UNITS * c + u - 1)
                    for tt in range(4):
                        for jj in range(2):
                            for b2 in range(2):
                                j, b = 2 * jp + jj, 2 * t + b2
                                last = pe.matmul(psS[u % 2][L * b2:L * b2 + L, jj, SW * tt:SW * (tt + 1)],
                                                 QS[32 * j:32 * j + 32, par, tt, b, :],
                                                 KS[32 * j:32 * j + 32, par, tt, b, :], start=True, stop=True)
                    last.then_inc(scored, 1)

                def turn(u):
                    g = UNITS * c + u - 1
                    pe.wait_ge(probs, g + 1)
                    wait(pe, turned_kept, g)
                    for q in range(4):
                        last = pe.transpose(psP[:, q], PR[:, (u - 1) % 2, 2 * q:2 * q + 2, :].rearrange("p a l -> p (a l)"),
                                            ident[:])
                    last.then_inc(turned, 1)

                def weigh(u):
                    v, vp = (u - 2) % UNITS, par if u >= 2 else prv
                    t, jp = v // 2, v % 2
                    pe.wait_ge(turned_kept, UNITS * c + u - 1)
                    if jp == 0:
                        wait(pe, out_read, TC * c + (u - 2) // 2)
                    for q in range(4):
                        for b2 in range(2):
                            last = pe.matmul(
                                psO[L * b2:L * b2 + L, 18 * (4 * jp + q):18 * (4 * jp + q + 1)],
                                PT[:, v % 2, q, L * b2:L * b2 + L], VB[:, vp, 2 * t + b2, 4 * jp + q, :],
                                start=True, stop=True)
                    last.then_inc(weighed, 1)

                for u in range(UNITS):
                    if scores:
                        score(u)
                    if (scores and u >= 1) or (u == 0 and finish):
                        turn(u)
                    names = ATTENTION.now(u, prepare, finish)
                    for name in names[:2]:
                        item(name)
                    if (scores and u >= 2) or (u < 2 and finish):
                        weigh(u)
                    for name in names[2:]:
                        item(name)

            run_bodies(pe, body)

        @block.scalar
        def _(act):
            act.wait_ge(folded, FOLDED)
            act.wait_ge(loaded, 16 * 9)

            def body(c, par, scores, prepare, finish):
                nxt = 1 - par

                def item(name):
                    if name in ("F mT", "F sel", "F y"):
                        return
                    b, n = spare_bank(c, name)
                    bank = spare[b]
                    act.wait_ge(filled[b], n)
                    if name == "A xT":
                        act.copy(xT[:, :, 0:L], bank[:].rearrange("p (b l) -> p b l", l=L)).then_inc(emptied[b], 1)
                    elif name == "A xS":
                        act.copy(xT[:, :, L:KW], bank[:, 0:BC * SELW].rearrange("p (b s) -> p b s", s=SELW)
                                 ).then_inc(emptied[b], 1)
                    elif name == "A q":
                        act.activation(qhi[:], bank[:].rearrange("p (b l) -> p b l", l=L), ACT.Identity,
                                       bias=bqs[:, 0:1]).then_inc(hi_made, 1)
                    elif name in ("A k0", "A k1"):
                        h = int(name[-1])
                        act.activation(khi[:, 4 * h:4 * h + 4], bank[:, 0:4 * KW].rearrange("p (b s) -> p b s", s=KW),
                                       ACT.Identity, bias=bkc[:, 0:1]).then_inc(hi_made, 1)
                    elif name == "A v":
                        for half in range(2):
                            r = slice(L * half, L * half + L)
                            last = act.copy(VB[r, nxt, :, :, (HD + 1) * half:(HD + 1) * half + HD],
                                            bank[r].rearrange("p (b h d) -> p b h d", b=BC, d=HD))
                        last.then_inc(emptied[b], 1)
                    elif name == "A vm":
                        act.copy(att[:, nxt], bank[:].rearrange("p (t d) -> p t d", t=TC)).then_inc(emptied[b], 1)
                    elif name[:4] == "A sq":
                        act.copy(QS[:, nxt, int(name[4])], bank[:].rearrange("p (b l) -> p b l", l=L)
                                 ).then_inc(emptied[b], 1)
                    elif name[:4] == "A sk":
                        t, h = int(name[4]), int(name[5])
                        act.copy(KS[:, nxt, t, 4 * h:4 * h + 4], bank[:, 0:4 * SW].rearrange("p (b s) -> p b s", s=SW)
                                 ).then_inc(emptied[b], 1)
                    elif name == "F aT":
                        act.copy(attT[:], bank[:]).then_inc(emptied[b], 1)
                    elif name == "F x1T":
                        act.copy(x1T[:], bank[:]).then_inc(emptied[b], 1)
                        act.wait_ge(emptied[b], n)
                        act.copy(XTh[:, bass.ds((c - 1) * CW, CW)], x1T[:]).then_inc(hi_kept, 1)

                for u in range(UNITS):
                    g = UNITS * c + u
                    if (scores and u >= 1) or (u == 0 and finish):
                        act.wait_ge(turned, g)
                        wait(act, weighed, g - 2)
                        act.copy(PT[:, (u - 1) % 2], psP[:]).then_inc(turned_kept, 1)
                    names = ATTENTION.now(u, prepare, finish)
                    for name in names[:2]:
                        item(name)
                    if scores:
                        act.wait_ge(shifted, g + 1)
                        act.activation(PR[:, u % 2], PR[:, u % 2], ACT.Exp).then_inc(probs, 1)
                    if u == 6 and finish:
                        act.wait_ge(shift_made, c)
                        act.wait_ge(x1_kept, c)
                        for t in range(TC):
                            last = act.activation(x1s[:, t], y[:, t], ACT.Identity, scale=rstd[:, t],
                                                  bias=shift[:, t])
                        last.then_inc(x1_made, 1)
                    for name in names[2:]:
                        item(name)

            run_bodies(act, body)

        @block.vector
        def _(dve):
            own = Own(dve, own_v)
            tt, ts, stt = dve.tensor_tensor, dve.tensor_scalar, dve.scalar_tensor_tensor
            dve.wait_ge(loaded, 16 * 9)
            dve.wait_ge(consts, 24)
            ts(Wqs[:], Wq[:], SCALE, None, ALU.mult).then_inc(folded, 1)
            ts(bqs[:], bqc[:], SCALE, None, ALU.mult).then_inc(folded, 1)
            dve.wait_ge(bias_through, 1)
            tt(bof[:], bof[:], psO[:, 0:D], ALU.add).then_inc(folded, 1)
            own.add(dve.tensor_copy(idf[:], idx[:]))
            own.add(dve.tensor_copy(lrowf[:], lrow[:]))
            own.settle()
            own.add(ts(neg[:], idf[:], 0.0, float(L), ALU.is_lt, ALU.mult))
            own.settle()
            own.add(tt(idf[:], idf[:], neg[:], ALU.add))
            own.settle()
            own.add(ts(idf[:], idf[:], 0.0, float(L - 1), ALU.max, ALU.min))
            own.settle()
            own.add(ts(hot[:], idf[:], lrowf[:, 0:1], None, ALU.is_equal))
            own.settle()
            own.add(dve.reduce_sum(cnt[:], hot[:], axis=X_AXIS))
            own.settle()
            for half in range(2):
                rows = slice(L * half, L * half + L)
                dve.tensor_copy(selbd[rows, half, 0:NS], hot[rows]).then_inc(folded, 1)
                ts(selbd[rows, half, NS:NS + 1], cnt[rows], 1.0 / NS, None, ALU.mult).then_inc(folded, 1)
                dve.memset(selbd[rows, half, NS + 1:NS + 2], 1.0 / L).then_inc(folded, 1)
            own.restart()

            def body(c, par, scores, prepare, finish):
                nxt = prv = 1 - par

                def unit(u):
                    s = psS[u % 2][:, :, 0:4 * SW].rearrange("p j (t k) -> p j t k", t=4)
                    dve.wait_ge(scored, UNITS * c + u + 1)
                    nm = nmax[:, u % 2].rearrange("p (j t a) -> p j t a", j=2, a=1)
                    sm = smax[:, u % 2].rearrange("p (j t a) -> p j t a", j=2, a=1)
                    own.add(dve.tensor_reduce(nm[:, :, :, 0], s[:, :, :, 0:L], X_AXIS, ALU.max, negate=True))
                    own.add(dve.tensor_reduce(sm[:, :, :, 0], s[:, :, :, L:L + NS], X_AXIS, ALU.max))
                    own.settle()
                    wait(dve, turned, UNITS * c + u - 1)
                    pr = PR[:, u % 2].rearrange("p (j t) l -> p j t l", j=2)
                    tt(pr, s[:, :, :, 0:L], nm.to_broadcast([P, 2, 4, L]), ALU.add).then_inc(shifted, 1)
                    m = M[:, par, 8 * u:8 * u + 8].rearrange("p (j t) -> p j t", j=2)
                    tt(m, sm[:, :, :, 0], s[:, :, :, SW - 1], ALU.subtract).then_inc(scores_read, 1)

                def read_out(u):
                    tile = (u - 4) // 2 % TC
                    dve.wait_ge(weighed, UNITS * c + u - 2)
                    dve.tensor_copy(O9[:, par if u >= 4 else prv, tile].rearrange("p h d -> p (h d)"),
                                    psO[:]).then_inc(out_read, 1)

                def low(name):
                    b, n = spare_bank(c, name)
                    dve.wait_ge(hi_made, 3 * (c + 1) + 1 + ("A q", "A k0", "A k1").index(name))
                    if name == "A q":
                        stt(qlo[:], spare[b][:].rearrange("p (b l) -> p b l", l=L), bqs[:, 0:1], qhi[:],
                            ALU.add, ALU.subtract).then_inc(emptied[b], 1)
                    else:
                        h = int(name[-1])
                        stt(klo[:, 4 * h:4 * h + 4], spare[b][:, 0:4 * KW].rearrange("p (b s) -> p b s", s=KW),
                            bkc[:, 0:1], khi[:, 4 * h:4 * h + 4], ALU.add, ALU.subtract).then_inc(emptied[b], 1)

                def took(name):
                    b, n = spare_bank(c, name)
                    dve.wait_ge(filled[b], n)
                    return spare[b], emptied[b]

                def take_measures():
                    bank, done = took("F mT")
                    own.add(dve.tensor_copy(top0[0:L, 0:L], bank[0:L, 0:L]))
                    own.add(dve.tensor_copy(top0[L:P, 0:L], bank[0:L, L:P]))
                    dve.tensor_copy(freeing[:], bank[0:1, 0:1]).then_inc(done, 1)

                def choose(first, last):
                    for r in range(first, last):
                        src = top1 if r else top0
                        own.settle()
                        own.add(dve.max(mx8[:], src[:]))
                        own.settle()
                        own.add(dve.match_replace(top1[:], mx8[:], src[:], -BIG))
                    if last == ROUNDS:
                        own.settle()
                        ts(chosen[:], top1[:, 0:L], -BIG, None, ALU.is_le).then_inc(chosen_made, 1)

                def take_choice():
                    bank, done = took("F sel")
                    own.add(dve.tensor_copy(selT[0:L], bank[0:L, 0:L]))
                    own.add(dve.tensor_copy(selT[L:P], bank[0:L, L:P]))
                    dve.tensor_copy(freeing[:], bank[0:1, 0:1]).then_inc(done, 1)

                def mix():
                    dve.wait_ge(out_read, TC * c)
                    own.add(dve.reciprocal(rden[:], O9[:, prv, :, :, HD]))
                    own.settle()
                    r = rden[:].rearrange("p t (h a) -> p t h a", a=1).to_broadcast([P, TC, H, HD])
                    own.add(tt(onorm[:], O9[:, prv, :, :, 0:HD], r, ALU.mult))
                    own.settle()
                    mask = selT[:].bitcast(U32).rearrange("p (h a) -> p h a", a=1).to_broadcast([P, TC * H, HD])
                    dve.copy_predicated(att[:, prv].rearrange("p t (h d) -> p (t h) d", d=HD), mask,
                                        onorm[:].rearrange("p t h d -> p (t h) d")).then_inc(mixed, 1)

                def residual():
                    bank, done = took("F y")
                    dve.wait_ge(xb_made, c)
                    tt(y[:], bank[:].rearrange("p (t d) -> p t d", t=TC), xb[:, prv], ALU.add).then_inc(done, 1)

                def variance():
                    b, n = spare_bank(c, "F y")
                    dve.wait_ge(emptied[b], n)
                    for t in range(TC):
                        own.add(dve.bn_stats(stats[:, t], y[:, t]))
                    own.settle()
                    for t in range(TC):
                        own.add(dve.bn_aggr(mv[:, t], stats[:, t]))
                    own.settle()
                    ts(nmean[:], mv[:, :, 0:1], -1.0, None, ALU.mult).then_inc(var_made, 1)
                    ts(vare[:], mv[:, :, 1:2], EPS, None, ALU.add).then_inc(var_made, 1)

                for u in range(UNITS):
                    if finish and u == 6:
                        residual()
                        variance()
                    if u % 2 == 0 and ((scores and u >= 4) or (finish and u <= 2)):
                        read_out(u)
                    if finish and u == 4:
                        take_choice()
                    if scores:
                        unit(u)
                    if finish and u == 0:
                        take_measures()
                        choose(0, 2)
                    if prepare and u == 1:
                        low("A q")
                        low("A k0")
                    if finish and u == 1:
                        choose(2, 3)
                    if prepare and u == 2:
                        low("A k1")
                    if finish and u == 2:
                        choose(3, ROUNDS)
                    if finish and u == 4:
                        mix()
                if own.n:
                    own.restart()

            run_bodies(dve, body)


E1, HID1 = 8, 256
U1 = E1 * HID1 // P
E2, F2 = 16, 64
LAG1 = 3
POOL1 = (11, 12, 13, 15)
GATED = Plan([[], [], [], ["F oT0", "F oT1"], [], [], [], [], [], ["F xT"], [], ["F rt", "A sum"], [], [], [], ["F cT"]])
PART = 32
PIECE = 4


def gated_experts(nc, k, ctx_w, itok, w_in, w_out, wr):
    with ExitStack() as ctx:
        def sb(name, shape, dt=F32):
            return ctx.enter_context(nc.sbuf_tensor(name, shape, dt))

        def ps(name, shape, dt=F32):
            return ctx.enter_context(nc.psum_tensor(name, shape, dt))

        def sem(name):
            return ctx.enter_context(nc.semaphore(name))

        X, XTh, XTl, ident, CWT = k.X, k.XTh, k.XTl, k.ident, k.CWT
        Wih, Wil = sb("Wih", [P, U1, P], F32R), sb("Wil", [P, U1, P], F32R)
        Woh, Wol = sb("Woh", [P, U1, P], F32R), sb("Wol", [P, U1, P], F32R)
        Wr = sb("Wr", [P, E2])
        identb = sb("identb", [P, P], BF16)
        row_of = sb("row_of", [P, E1, 2 * E1])
        pick = sb("pick", [3 * PART, 2, E1, P], BF16)
        pick_row = sb("pick_row", [3 * PART, 2 * E1, 1])
        wts, ids = sb("wts", [P, 2, TC, L]), sb("ids", [P, 2, TC, L], I32)
        wm, wm_done = sb("wm", [P, E1, TC, L]), sb("wm_done", [1, 1])
        freeing = sb("freeing2", [1, 1])
        gr = sb("gr", [P, TC * L])
        GT = sb("GT", [3 * PART, 2, TC * L], BF16)
        gs = sb("gs", [P, 2, CW])
        hg = sb("hg", [P, 4, CW])
        stage = hg[:].rearrange("p n (a q) -> p n a q", a=PIECE)
        hh, hl = sb("hh", [P, 4, CW], F32R), sb("hl", [P, 4, CW], F32R)
        oT = sb("oT", [P, CW])
        y, x2s = sb("y2", [P, TC, D]), sb("x2s", [P, TC, D])
        stats, mv = sb("stats2", [P, TC, 6]), sb("mv2", [P, TC, 2])
        vare, rstd = sb("vare2", [P, TC, 1]), sb("rstd2", [P, TC, 1])
        nmean, shift = sb("nmean2", [P, TC, 1]), sb("shift2", [P, TC, 1])
        x2T = sb("x2T", [P, CW])
        lmax, lsum, lrec = (sb(n, [P, TC, 1]) for n in ("lmax", "lsum", "lrec"))
        lg = sb("lg", [P, TC, E2])
        pr0, pr1 = sb("pr0", [P, TC, E2 + 6]), sb("pr1", [P, TC, E2 + 6])
        mx8 = sb("mx8b", [P, TC, 8])
        cw, cwr = sb("cw", [P, TC, E2]), sb("cwr", [P, TC, E2])
        cw3 = sb("cw3", [P, TC, 3, E2], BF16)

        psH = [ps(f"psH{i}", [P, 512]) for i in range(2)]
        psG = [ps(f"psG{i}", [P, 512]) for i in range(2)]
        psO = [ps(f"psOut{i}", [P, 512]) for i in range(2)]
        spare = [ps(f"aux{i}", [P, 512]) for i in range(2)]

        loaded = sem("router_loaded")
        staged = [sem(f"weights_staged{i}") for i in range(4)]
        w_hi = sem("weights_high_made")
        w_lo = sem("weights_low_made")
        consts, spread_consts = sem("constants_made2"), sem("wide_constants_made")
        own_v, own_p = sem("vector_results2"), sem("pool_results2")
        gates_loaded = [sem(f"gates_loaded{i}") for i in range(2)]
        masked = sem("gates_masked")
        gates_high = sem("gates_high_part_made")
        gates_made = sem("gates_made")
        filled = [sem(f"aux{i}_filled") for i in range(2)]
        emptied = [sem(f"aux{i}_emptied") for i in range(2)]
        hidden = sem("hidden_filled")
        spread = sem("gate_spread")
        gs_kept = sem("gate_in_sbuf")
        gated = sem("hidden_gated")
        hi_made = sem("hidden_high_made")
        lo_made = {"vector": sem("hidden_low_by_vector"), "gpsimd": sem("hidden_low_by_gpsimd")}
        added = sem("unit_added")
        oT_kept = sem("output_in_sbuf")
        var_made = sem("variance_made2")
        rstd_made, shift_made = sem("rstd_made2"), sem("shift_made2")
        x2_made = sem("x2_made")
        x2_kept = sem("x2_kept")
        xh_kept, xl_kept = sem("x2_high_kept"), sem("x2_low_kept")
        shifted = sem("logits_shifted")
        raised = sem("logits_raised")
        routed = sem("routed")

        block = ctx.enter_context(nc.Block())
        pieces = [(w, i) for i in range(U1 // PIECE) for w in (0, 1)]

        def low_done(engine, c, v):
            mine = [u for u in range(U1) if (u in POOL1) == (v in POOL1)]
            wait(engine, lo_made["gpsimd" if v in POOL1 else "vector"], len(mine) * c + mine.index(v) + 1)

        @block.sync
        def _(sp):
            def load(c, par):
                for src, dst in ((ctx_w, wts), (itok, ids)):
                    for b2 in range(2):
                        part = src[bass.ds(BC * c, BC)].rearrange("(t b) k s -> b k t s", b=2)[b2]
                        sp.dma_start(dst[L * b2:L * b2 + L, par], part).then_inc(gates_loaded[par], 16)

            load(0, 0)
            load(1, 1)
            for n, (w, i) in enumerate(pieces):
                if n >= 4:
                    sp.wait_ge(w_lo, n - 3)
                src = (w_in, w_out)[w]
                sp.dma_start(stage[:, n % 4], src[:, PIECE * i:PIECE * (i + 1), :]).then_inc(staged[n % 4], 16)
            sp.dma_start(Wr[:], wr).then_inc(loaded, 16)

            with sp.Fori(0, (NCH - 2) // 2) as pair:
                sp.wait_ge(masked, 2 * pair + 1)
                load(2 * pair + 2, 0)
                sp.wait_ge(masked, 2 * pair + 2)
                load(2 * pair + 3, 1)

        @block.gpsimd
        def _(pool):
            pool.memset(row_of[:], 0.0).then_inc(consts, 1)
            pool.memset(pr0[:], BIG).then_inc(consts, 1)
            pool.memset(pick_row[:], 0.0).then_inc(consts, 1)
            pool.wait_ge(consts, 3)
            for half in range(2):
                v = row_of[L * half:L * half + L, :, E1 * half:E1 * half + E1]
                pool.affine_select(out=v, in_=v, compare_op=ALU.not_equal, fill=1.0, base=0,
                                   pattern=[[1, E1], [-1, E1]], channel_multiplier=0).then_inc(consts, 1)
                pool.wait_ge(consts, 4 + half)
            for part in range(3):
                v = pick_row[:, :, 0]
                pool.affine_select(out=v, in_=v, compare_op=ALU.not_equal, fill=1.0, base=-PART * part,
                                   pattern=[[-1, 2 * E1]], channel_multiplier=1).then_inc(consts, 1)
                pool.wait_ge(consts, 6 + part)
            own = Own(pool, own_p)

            def body(c, par, scores, prepare, finish):
                n = 1 - par
                if prepare:
                    pool.wait_ge(gates_loaded[n], 2 * loads_of(c + 1, n))
                    wait(pool, gates_made, c + 1)
                    own.add(pool.tensor_tensor(wm_done[:], k.minus_half[0:1, 0], k.minus_half[0:1, 0], ALU.add))
                    own.settle()
                    for e in range(E1):
                        own.add(pool.tensor_scalar(wm[:, e], ids[:, n], float(e), None, ALU.is_equal))
                for u in range(U1):
                    if scores and u in POOL1:
                        wait(pool, added, U1 * c + u - 3)
                        pool.wait_ge(hi_made, U1 * c + u + 1)
                        pool.tensor_tensor(hl[:, u % 4], hg[:, u % 4], hh[:, u % 4].bitcast(F32), ALU.subtract
                                           ).then_inc(lo_made["gpsimd"], 1)
                    if u == 5 and finish:
                        pool.wait_ge(var_made, 2 * c)
                        pool.tensor_tensor(rstd[:], vare[:], k.minus_half[:, 0:TC, :], ALU.pow).then_inc(rstd_made, 1)
                        pool.wait_ge(rstd_made, c)
                        pool.tensor_tensor(shift[:], nmean[:], rstd[:], ALU.mult).then_inc(shift_made, 1)
                    if u == 6 and prepare:
                        own.settle()
                        for e in range(E1):
                            last = pool.tensor_tensor(wm[:, e], wm[:, e], wts[:, n], ALU.mult)
                        last.then_inc(masked, 1)
                        own.restart()
                    if u == 9 and finish:
                        chunk = bass.ds((c - 1) * CW, CW)
                        pool.wait_ge(xh_kept, c)
                        pool.tensor_tensor(XTl[:, chunk], x2T[:], XTh[:, chunk].bitcast(F32), ALU.subtract
                                           ).then_inc(xl_kept, 1)

            run_bodies(pool, body)
            pool.wait_ge(xl_kept, NCH)

        @block.tensor
        def _(pe):
            pe.wait_ge(consts, 8)
            pe.wait_ge(spread_consts, 4)
            pe.wait_ge(loaded, 16)
            pe.wait_ge(w_lo, len(pieces))

            def body(c, par, scores, prepare, finish):
                nxt = prv = 1 - par

                def kept(name):
                    b, n = GATED.at(c, name)
                    pe.wait_ge(emptied[b], n)

                def item(name):
                    b, n = GATED.at(c, name)
                    bank = spare[b]
                    wait(pe, emptied[b], n - 1)
                    if name == "A sum":
                        pe.wait_ge(masked, c + 2)
                        for e in range(E1):
                            last = pe.matmul(bank[0:2 * E1, 0:TC * L], row_of[:, e],
                                             wm[:, e].rearrange("p t l -> p (t l)"),
                                             start=(e == 0), stop=(e == E1 - 1))
                    elif name in ("F oT0", "F oT1"):
                        pe.wait_ge(oT_kept, c)
                        for t in range(TC // 2):
                            tile = TC // 2 * int(name[-1]) + t
                            last = pe.transpose(bank[:, P * t:P * t + P], oT[:, P * tile:P * tile + P], ident[:])
                    elif name == "F xT":
                        pe.wait_ge(x2_made, 2 * c)
                        for t in range(TC):
                            last = pe.transpose(bank[:, P * t:P * t + P], x2s[:, t], ident[:])
                    elif name == "F rt":
                        kept("F xT")
                        for t in range(TC):
                            last = pe.matmul(bank[:, E2 * t:E2 * t + E2], x2T[:, P * t:P * t + P], Wr[:],
                                             start=True, stop=True)
                    elif name == "F cT":
                        pe.wait_ge(routed, c)
                        for t in range(TC):
                            last = pe.matmul(bank[0:3 * E2, P * t:P * t + P],
                                             cw3[:, t].rearrange("p a e -> p (a e)"), identb[:],
                                             start=True, stop=True)
                    last.then_inc(filled[b], 1)

                def project(u):
                    wait(pe, gated, U1 * c + u - 1)
                    chunk = bass.ds(c * CW, CW)
                    bank = psH[u % 2]
                    pe.matmul(bank[:], Wih[:, u], XTh[:, chunk], start=True, stop=False)
                    pe.matmul(bank[:], Wih[:, u], XTl[:, chunk], start=False, stop=False)
                    pe.matmul(bank[:], Wil[:, u], XTh[:, chunk], start=False, stop=True).then_inc(hidden, 1)

                def spread_gate(u):
                    e = (u + 1) // 2
                    g, buf = (U1 // 2 * c + e, par) if u < U1 - 1 else (U1 // 2 * (c + 1), nxt)
                    e %= E1
                    if e == 0:
                        pe.wait_ge(gates_made, c + 2)
                    wait(pe, gs_kept, g - 1)
                    tokens = psG[e % 2][:].rearrange("p (t b l) -> p b t l", b=2, l=L)
                    for b2 in range(2):
                        last = pe.matmul(tokens[:, b2], pick[:, b2, e], GT[:, buf], start=True, stop=True)
                    last.then_inc(spread, 1)

                def add(u):
                    v, o = (u - LAG1) % U1, psO[par if u >= LAG1 else prv]
                    low_done(pe, c if u >= LAG1 else c - 1, v)
                    n = v % 4
                    pe.matmul(o[:], Woh[:, v], hh[:, n], start=(v == 0), stop=False)
                    pe.matmul(o[:], Wol[:, v], hh[:, n], start=False, stop=False)
                    pe.matmul(o[:], Woh[:, v], hl[:, n], start=False, stop=(v == U1 - 1)).then_inc(added, 1)

                for u in range(U1):
                    if scores:
                        project(u)
                    if u % 2 == 1 and (scores if u < U1 - 1 else prepare):
                        spread_gate(u)
                    if (scores and u >= LAG1) or (u < LAG1 and finish):
                        add(u)
                    for name in GATED.now(u, prepare, finish):
                        item(name)

            run_bodies(pe, body)

        @block.scalar
        def _(act):
            for n, (w, i) in enumerate(pieces):
                act.wait_ge(staged[n % 4], 16 * (n // 4 + 1))
                act.copy((Wih, Woh)[w][:, PIECE * i:PIECE * (i + 1)], stage[:, n % 4]).then_inc(w_hi, 1)
            act.wait_ge(spread_consts, 4)

            def body(c, par, scores, prepare, finish):
                nxt = prv = 1 - par

                def copied(name):
                    b, n = GATED.at(c, name)
                    act.wait_ge(filled[b], n)
                    return spare[b], emptied[b]

                def high(u):
                    g = U1 * c + u
                    act.wait_ge(gated, g + 1)
                    wait(act, added, g - 3)
                    act.copy(hh[:, u % 4], hg[:, u % 4]).then_inc(hi_made, 1)

                def keep_gate(u):
                    g = U1 // 2 * c + (u + 1) // 2
                    act.wait_ge(spread, g + 1)
                    wait(act, gated, 2 * g - 2)
                    act.copy(gs[:, (u + 1) // 2 % 2], psG[(u + 1) // 2 % 2][:]).then_inc(gs_kept, 1)

                for u in range(U1):
                    if u == LAG1 and finish:
                        act.wait_ge(added, U1 * c)
                        act.copy(oT[:], psO[prv][:]).then_inc(oT_kept, 1)
                    if u % 2 == 1 and (scores if u < U1 - 1 else prepare):
                        keep_gate(u)
                    if u in (7, 8) and finish:
                        act.wait_ge(shift_made, c)
                        for t in range(TC // 2 * (u - 7), TC // 2 * (u - 6)):
                            last = act.activation(x2s[:, t], y[:, t], ACT.Identity, scale=rstd[:, t],
                                                  bias=shift[:, t])
                        last.then_inc(x2_made, 1)
                    if u == 12 and prepare:
                        bank, _ = copied("A sum")
                        act.copy(GT[0:2 * E1, nxt], bank[0:2 * E1, 0:TC * L]).then_inc(gates_high, 1)
                    if u == 10 and finish:
                        bank, done = copied("F xT")
                        act.copy(x2T[:], bank[:]).then_inc(done, 1)
                        b, n = GATED.at(c, "F xT")
                        act.wait_ge(emptied[b], n)
                        act.copy(XTh[:, bass.ds((c - 1) * CW, CW)], x2T[:]).then_inc(xh_kept, 1)
                    if scores:
                        high(u)
                    if u == 12 and finish:
                        act.wait_ge(x2_made, 2 * c)
                        act.copy(X[:, bass.ds((c - 1) * TC, TC), :], x2s[:]).then_inc(x2_kept, 1)
                        act.wait_ge(shifted, c)
                        act.activation(lg[:], lg[:], ACT.Exp).then_inc(raised, 1)
                    if u == 15 and finish:
                        bank, done = copied("F cT")
                        act.copy(CWT[0:3 * E2, bass.ds((c - 1) * CW, CW)], bank[0:3 * E2]).then_inc(done, 1)

            run_bodies(act, body)
            act.wait_ge(x2_kept, NCH)

        @block.vector
        def _(dve):
            own = Own(dve, own_v)
            tt, ts, stt = dve.tensor_tensor, dve.tensor_scalar, dve.scalar_tensor_tensor
            dve.memset(CWT[:], 0.0).then_inc(spread_consts, 1)
            dve.memset(GT[:], 0.0).then_inc(spread_consts, 1)
            dve.wait_ge(consts, 8)
            dve.tensor_copy(identb[:], ident[:]).then_inc(spread_consts, 1)
            dve.tensor_copy(pick[:].rearrange("p b e m -> p (b e) m"), pick_row[:].to_broadcast([3 * PART, 2 * E1, P])
                            ).then_inc(spread_consts, 1)
            for n, (w, i) in enumerate(pieces):
                tiles = slice(PIECE * i, PIECE * (i + 1))
                dve.wait_ge(w_hi, n + 1)
                tt((Wil, Wol)[w][:, tiles], stage[:, n % 4], (Wih, Woh)[w][:, tiles].bitcast(F32), ALU.subtract
                   ).then_inc(w_lo, 1)
            dve.wait_ge(spread_consts, 4)

            def body(c, par, scores, prepare, finish):
                nxt = prv = 1 - par

                def took(name):
                    b, n = GATED.at(c, name)
                    dve.wait_ge(filled[b], n)
                    return spare[b], emptied[b]

                def gate(u):
                    g = U1 * c + u
                    if u % 2 == 0:
                        dve.wait_ge(gs_kept, U1 // 2 * c + u // 2 + 1)
                    if u >= 4:
                        low_done(dve, c, u - 4)
                    else:
                        low_done(dve, c - 1, u - 4 + U1)
                    dve.wait_ge(hidden, g + 1)
                    stt(hg[:, u % 4], psH[u % 2][:], 0.0, gs[:, u // 2 % 2], ALU.max, ALU.mult).then_inc(gated, 1)

                def low(u):
                    g = U1 * c + u
                    wait(dve, added, g - 3)
                    dve.wait_ge(hi_made, g + 1)
                    tt(hl[:, u % 4], hg[:, u % 4], hh[:, u % 4].bitcast(F32), ALU.subtract
                       ).then_inc(lo_made["vector"], 1)

                def step(u, place):
                    at = (u, place)
                    if at == (12, 2) and prepare:
                        bank, _ = took("A sum")
                        dve.wait_ge(gates_high, c + 2)
                        own.add(tt(GT[PART:PART + 2 * E1, nxt], bank[0:2 * E1, 0:TC * L], GT[0:2 * E1, nxt],
                                   ALU.subtract))
                    elif at == (13, 0) and prepare:
                        bank, done = took("A sum")
                        tt(gr[PART:PART + 2 * E1], bank[0:2 * E1, 0:TC * L], GT[0:2 * E1, nxt], ALU.subtract
                           ).then_inc(done, 1)
                    elif at == (13, 1) and prepare:
                        b, n = GATED.at(c, "A sum")
                        dve.wait_ge(emptied[b], n)
                        tt(GT[2 * PART:2 * PART + 2 * E1, nxt], gr[PART:PART + 2 * E1],
                           GT[PART:PART + 2 * E1, nxt], ALU.subtract).then_inc(gates_made, 1)
                    if not finish:
                        return
                    if at == (4, 1):
                        for half, name in enumerate(("F oT0", "F oT1")):
                            bank, done = took(name)
                            tiles = TC // 2
                            tt(y[:, tiles * half:tiles * (half + 1)],
                               bank[:, 0:tiles * D].rearrange("p (t d) -> p t d", t=tiles),
                               X[:, bass.ds((c - 1) * TC + tiles * half, tiles), :], ALU.add).then_inc(done, 1)
                    elif at == (4, 2):
                        for name in ("F oT0", "F oT1"):
                            b, n = GATED.at(c, name)
                            dve.wait_ge(emptied[b], n)
                        for t in range(TC):
                            own.add(dve.bn_stats(stats[:, t], y[:, t]))
                    elif at == (5, 1):
                        own.settle()
                        for t in range(TC):
                            own.add(dve.bn_aggr(mv[:, t], stats[:, t]))
                    elif at == (5, 2):
                        own.settle()
                        ts(nmean[:], mv[:, :, 0:1], -1.0, None, ALU.mult).then_inc(var_made, 1)
                        ts(vare[:], mv[:, :, 1:2], EPS, None, ALU.add).then_inc(var_made, 1)
                    elif at == (12, 0):
                        bank, _ = took("F rt")
                        s = bank[:, 0:TC * E2].rearrange("p (t e) -> p t e", e=E2)
                        own.add(dve.tensor_reduce(lmax[:, :, 0], s, X_AXIS, ALU.max, negate=True))
                    elif at == (12, 1):
                        bank, done = took("F rt")
                        s = bank[:, 0:TC * E2].rearrange("p (t e) -> p t e", e=E2)
                        own.settle()
                        tt(lg[:], s, lmax[:].to_broadcast([P, TC, E2]), ALU.add).then_inc(shifted, 1)
                        dve.tensor_copy(freeing[:], bank[0:1, 0:1]).then_inc(done, 1)
                    elif at == (13, 0):
                        dve.wait_ge(raised, c)
                        own.add(dve.reduce_sum(lsum[:, :, 0], lg[:], axis=X_AXIS))
                        own.settle()
                        own.add(dve.reciprocal(lrec[:], lsum[:]))
                        own.settle()
                        own.add(tt(pr0[:, :, 0:E2], lg[:], lrec[:].to_broadcast([P, TC, E2]), ALU.mult))
                    elif at == (13, 1):
                        own.settle()
                        for t in range(TC):
                            own.add(dve.max(mx8[:, t], pr0[:, t]))
                        own.settle()
                        for t in range(TC):
                            own.add(dve.match_replace(pr1[:, t], mx8[:, t], pr0[:, t], -BIG))
                    elif at == (13, 2):
                        own.settle()
                        own.add(stt(cw[:], pr1[:, :, 0:E2], -BIG, pr0[:, :, 0:E2], ALU.is_le, ALU.mult))
                        own.settle()
                        own.add(dve.tensor_copy(cw3[:, :, 0], cw[:]))
                    elif at == (14, 0):
                        own.settle()
                        own.add(tt(cw3[:, :, 1], cw[:], cw3[:, :, 0], ALU.subtract))
                        own.add(tt(cwr[:], cw[:], cw3[:, :, 0], ALU.subtract))
                        own.settle()
                        tt(cw3[:, :, 2], cwr[:], cw3[:, :, 1], ALU.subtract).then_inc(routed, 1)

                for u in range(U1):
                    step(u, 0)
                    if scores:
                        gate(u)
                    step(u, 1)
                    if ((scores and u >= 1) or (u == 0 and finish)) and (u - 1) % U1 not in POOL1:
                        low(u - 1)
                    step(u, 2)
                if own.n:
                    own.restart()

            run_bodies(dve, body)


U2 = E2 * F2 // P + 1
PIECE2 = 3
LAG2 = 3
RING2 = 6
POOL2 = (1, 4, 7)


def routed_experts(nc, k, w_gate, w_up, w_down, out):
    with ExitStack() as ctx:
        def sb(name, shape, dt=F32):
            return ctx.enter_context(nc.sbuf_tensor(name, shape, dt))

        def ps(name, shape, dt=F32):
            return ctx.enter_context(nc.psum_tensor(name, shape, dt))

        def sem(name):
            return ctx.enter_context(nc.semaphore(name))

        X, XTh, XTl, ident, CWT = k.X, k.XTh, k.XTl, k.ident, k.CWT
        parts = {}
        for name in ("gate", "up", "down"):
            parts[name] = (sb(f"W{name}h", [P, U2, P], F32R), sb(f"W{name}l", [P, U2, P], F32R))
        pick = sb("pick3", [P, U2 - 1, 2, F2], BF16)
        sg, tu, hg = sb("sg", [P, 2, CW]), sb("tu", [P, 2, CW]), sb("hg3", [P, 3, CW])
        stage = [t[:, n, 0:PIECE2 * P].rearrange("p (a q) -> p a q", a=PIECE2)
                 for t, m in ((hg, 3), (tu, 2), (sg, 2)) for n in range(m)]
        STAGES = len(stage)
        hh, hl = sb("hh3", [P, RING2, CW], F32R), sb("hl3", [P, RING2, CW], F32R)
        oT = sb("oT3", [P, CW])
        y, x3s = sb("y3", [P, TC, D]), sb("x3s", [P, 2, TC, D])
        stats, mv = sb("stats3", [P, TC, 6]), sb("mv3", [P, TC, 2])
        vare, rstd = sb("vare3", [P, TC, 1]), sb("rstd3", [P, TC, 1])
        nmean, shift = sb("nmean3", [P, TC, 1]), sb("shift3", [P, TC, 1])

        psg = [ps(f"psgate{i}", [P, 512]) for i in range(2)]
        psu = [ps(f"psup{i}", [P, 512]) for i in range(2)]
        psc = ps("psweight", [P, 512])
        psO = [ps(f"psdown{i}", [P, 512]) for i in range(2)]
        psT = ps("psturn", [P, 512])

        staged = [sem(f"experts_staged{i}") for i in range(STAGES)]
        w_hi, w_lo = sem("experts_high_made"), sem("experts_low_made")
        consts = sem("constants_made3")
        own_v = sem("vector_results3")
        gate_up = sem("gate_and_up_filled")
        weight = sem("weight_spread")
        silu_made = sem("silu_made")
        gated = sem("hidden_weighed")
        hi_made = sem("hidden_high_made3")
        lo_made = {"vector": sem("hidden_low_by_vector3"), "gpsimd": sem("hidden_low_by_gpsimd3")}
        added = sem("unit_added3")
        oT_kept = sem("output_in_sbuf3")
        turned = sem("output_turned")
        y_made = sem("residual_made3")
        var_made, rstd_made, shift_made = sem("variance_made3"), sem("rstd_made3"), sem("shift_made3")
        x3_made = sem("x3_made")
        stored = [sem(f"x3_stored{i}") for i in range(2)]

        block = ctx.enter_context(nc.Block())
        pieces = [(name, i) for i in range(U2 // PIECE2) for name in ("gate", "up", "down")]
        sources = {"gate": w_gate, "up": w_up, "down": w_down}

        def low_done(engine, c, v):
            mine = [u for u in range(U2) if (u in POOL2) == (v in POOL2)]
            wait(engine, lo_made["gpsimd" if v in POOL2 else "vector"], len(mine) * c + mine.index(v) + 1)

        def ring(par, v):
            return (U2 * par + v) % RING2

        def run(engine, body):
            body(0, 0, scores=True, finish=False)
            with engine.Fori(0, (NCH - 2) // 2) as pair:
                body(2 * pair + 1, 1, scores=True, finish=True)
                body(2 * pair + 2, 0, scores=True, finish=True)
            body(NCH - 1, 1, scores=True, finish=True)
            body(NCH, 0, scores=False, finish=True)

        @block.sync
        def _(sp):
            for n, (name, i) in enumerate(pieces):
                if n >= STAGES:
                    sp.wait_ge(w_lo, n - STAGES + 1)
                sp.dma_start(stage[n % STAGES], sources[name][:, PIECE2 * i:PIECE2 * (i + 1), :]
                             ).then_inc(staged[n % STAGES], 16)

            def body(c, par, scores, finish):
                if finish:
                    prv = 1 - par
                    sp.wait_ge(x3_made, c)
                    dst = out[bass.ds(BC * (c - 1), BC)].rearrange("(t b) l d -> b l t d", b=2)
                    for b2 in range(2):
                        sp.dma_start(dst[b2], x3s[L * b2:L * b2 + L, prv]).then_inc(stored[prv], 16)

            run(sp, body)
            for par in range(2):
                sp.wait_ge(stored[par], 32 * (NCH // 2 + 1))

        @block.gpsimd
        def _(pool):
            for par in range(2):
                pool.memset(x3s[:, par], 0.0).then_inc(stored[par], 32)
            pool.memset(pick[:], 0.0).then_inc(consts, 1)
            pool.wait_ge(consts, 1)
            for part in range(3):
                pool.affine_select(out=pick[:], in_=pick[:], compare_op=ALU.not_equal, fill=1.0, base=-E2 * part,
                                   pattern=[[-2, U2 - 1], [-1, 2], [0, F2]], channel_multiplier=1).then_inc(consts, 1)
                pool.wait_ge(consts, 2 + part)

            def body(c, par, scores, finish):
                for j in range(U2):
                    if scores and j in POOL2:
                        n = ring(par, j)
                        wait(pool, added, U2 * c + j - RING2 + 1)
                        pool.wait_ge(hi_made, U2 * c + j + 1)
                        pool.tensor_tensor(hl[:, n], hg[:, j % 3], hh[:, n].bitcast(F32), ALU.subtract
                                           ).then_inc(lo_made["gpsimd"], 1)
                    if j == 6 and finish:
                        pool.wait_ge(var_made, 2 * c)
                        pool.tensor_tensor(rstd[:], vare[:], k.minus_half[:, 0:TC, :], ALU.pow).then_inc(rstd_made, 1)
                        pool.wait_ge(rstd_made, c)
                        pool.tensor_tensor(shift[:], nmean[:], rstd[:], ALU.mult).then_inc(shift_made, 1)

            run(pool, body)
            pool.wait_ge(shift_made, NCH)

        @block.tensor
        def _(pe):
            pe.wait_ge(consts, 4)
            pe.wait_ge(w_lo, len(pieces))

            def body(c, par, scores, finish):
                prv = 1 - par

                def three(bank, w, j, hi, lo, start, stop):
                    wh, wl = parts[w]
                    pe.matmul(bank, wh[:, j], hi, start=start, stop=False)
                    pe.matmul(bank, wl[:, j], hi, start=False, stop=False)
                    return pe.matmul(bank, wh[:, j], lo, start=False, stop=stop)

                def project(j):
                    g, b = U2 * c + j, (par + j) % 2
                    chunk = bass.ds(c * CW, CW)
                    wait(pe, silu_made, g - 1)
                    three(psg[b][:], "gate", j, XTh[:, chunk], XTl[:, chunk], True, True)
                    wait(pe, gated, g - 1)
                    three(psu[b][:], "up", j, XTh[:, chunk], XTl[:, chunk], True, True).then_inc(gate_up, 1)

                def spread(j):
                    wait(pe, gated, U2 * c + j)
                    pe.matmul(psc[:], pick[:, j].rearrange("p a f -> p (a f)"), CWT[:, bass.ds(c * CW, CW)],
                              start=True, stop=True).then_inc(weight, 1)

                def add(j):
                    v, vp = (j - LAG2) % U2, par if j >= LAG2 else prv
                    n, o = ring(vp, v), psO[vp]
                    low_done(pe, c if j >= LAG2 else c - 1, v)
                    three(o[:], "down", v, hh[:, n], hl[:, n], v == 0, v == U2 - 1).then_inc(added, 1)

                for j in range(U2):
                    if scores:
                        project(j)
                    if (scores and j >= LAG2) or (j < LAG2 and finish):
                        add(j)
                    if scores and j < U2 - 1:
                        spread(j)
                    if j == LAG2 + 1 and finish:
                        pe.wait_ge(oT_kept, c)
                        for t in range(TC):
                            last = pe.transpose(psT[:, P * t:P * t + P], oT[:, P * t:P * t + P], ident[:])
                        last.then_inc(turned, 1)

            run(pe, body)

        @block.scalar
        def _(act):
            for n, (name, i) in enumerate(pieces):
                act.wait_ge(staged[n % STAGES], 16 * (n // STAGES + 1))
                act.copy(parts[name][0][:, PIECE2 * i:PIECE2 * (i + 1)], stage[n % STAGES]).then_inc(w_hi, 1)

            def body(c, par, scores, finish):
                prv = 1 - par

                def silu(j):
                    g, b = U2 * c + j, (par + j) % 2
                    act.wait_ge(gate_up, g + 1)
                    wait(act, gated, g - 1)
                    act.activation(sg[:, b], psg[b][:], ACT.Silu).then_inc(silu_made, 1)

                def high(j):
                    g, v = U2 * c + j - 1, (j - 1) % U2
                    act.wait_ge(gated, g + 1)
                    wait(act, added, g - RING2 + 1)
                    act.copy(hh[:, ring(par if j else prv, v)], hg[:, v % 3]).then_inc(hi_made, 1)

                for j in range(U2):
                    if scores:
                        silu(j)
                    if (scores and j >= 1) or (j == 0 and finish):
                        high(j)
                    if j == LAG2 and finish:
                        act.wait_ge(added, U2 * c)
                        act.copy(oT[:], psO[prv][:]).then_inc(oT_kept, 1)
                    if j == U2 - 1 and finish:
                        act.wait_ge(shift_made, c)
                        act.wait_ge(stored[prv], 16 * (c - 1 - prv) + 32)
                        for t in range(TC):
                            last = act.activation(x3s[:, prv, t], y[:, t], ACT.Identity, scale=rstd[:, t],
                                                  bias=shift[:, t])
                        last.then_inc(x3_made, 1)

            run(act, body)

        @block.vector
        def _(dve):
            own = Own(dve, own_v)
            tt, ts = dve.tensor_tensor, dve.tensor_scalar
            for n, (name, i) in enumerate(pieces):
                dve.wait_ge(w_hi, n + 1)
                wh, wl = parts[name]
                tiles = slice(PIECE2 * i, PIECE2 * (i + 1))
                tt(wl[:, tiles], stage[n % STAGES], wh[:, tiles].bitcast(F32), ALU.subtract).then_inc(w_lo, 1)

            def body(c, par, scores, finish):
                prv = 1 - par

                def weigh(j):
                    g, b, n = U2 * c + j, (par + j) % 2, j % 3
                    dve.wait_ge(silu_made, g + 1)
                    if j >= 3:
                        low_done(dve, c, j - 3)
                    else:
                        low_done(dve, c - 1, j - 3 + U2)
                    if j == U2 - 1:
                        tt(hg[:, n], sg[:, b], psu[b][:], ALU.mult).then_inc(gated, 1)
                    else:
                        own.add(tt(tu[:, b], sg[:, b], psu[b][:], ALU.mult))
                        own.settle()
                        dve.wait_ge(weight, (U2 - 1) * c + j + 1)
                        tt(hg[:, n], tu[:, b], psc[:], ALU.mult).then_inc(gated, 1)

                def low(j):
                    g, v = U2 * c + j - 1, (j - 1) % U2
                    n = ring(par if j else prv, v)
                    wait(dve, added, g - RING2 + 1)
                    dve.wait_ge(hi_made, g + 1)
                    tt(hl[:, n], hg[:, v % 3], hh[:, n].bitcast(F32), ALU.subtract).then_inc(lo_made["vector"], 1)

                def residual():
                    dve.wait_ge(turned, c)
                    tt(y[:], psT[:].rearrange("p (t d) -> p t d", t=TC), X[:, bass.ds((c - 1) * TC, TC), :],
                       ALU.add).then_inc(y_made, 1)

                def variance():
                    dve.wait_ge(y_made, c)
                    for t in range(TC):
                        own.add(dve.bn_stats(stats[:, t], y[:, t]))
                    own.settle()
                    for t in range(TC):
                        own.add(dve.bn_aggr(mv[:, t], stats[:, t]))
                    own.settle()
                    ts(nmean[:], mv[:, :, 0:1], -1.0, None, ALU.mult).then_inc(var_made, 1)
                    ts(vare[:], mv[:, :, 1:2], EPS, None, ALU.add).then_inc(var_made, 1)

                for j in range(U2):
                    if scores:
                        weigh(j)
                    if ((scores and j >= 1) or (j == 0 and finish)) and (j - 1) % U2 not in POOL2:
                        low(j)
                    if j == 5 and finish:
                        residual()
                    if j == 6 and finish:
                        variance()
                if own.n:
                    own.restart()

            run(dve, body)


class Kept:
    pass


def setup(nc, ctx):
    k = Kept()
    k.X = ctx.enter_context(nc.sbuf_tensor("X", [P, NCH * TC, D], F32))
    k.XTh = ctx.enter_context(nc.sbuf_tensor("XTh", [P, NCH * CW], F32R))
    k.XTl = ctx.enter_context(nc.sbuf_tensor("XTl", [P, NCH * CW], F32R))
    k.ident = ctx.enter_context(nc.sbuf_tensor("ident", [P, P], F32))
    k.minus_half = ctx.enter_context(nc.sbuf_tensor("minus_half", [P, TC, 1], F32))
    made = ctx.enter_context(nc.semaphore("identity_made"))
    with nc.Block() as block:
        @block.gpsimd
        def _(pool):
            pool.memset(k.minus_half[:], -0.5).then_inc(made, 1)
            pool.memset(k.ident[:], 0.0).then_inc(made, 1)
            pool.wait_ge(made, 2)
            pool.affine_select(out=k.ident[:], in_=k.ident[:], compare_op=ALU.not_equal, fill=1.0, base=0,
                               pattern=[[-1, P]], channel_multiplier=1).then_inc(made, 1)
            pool.wait_ge(made, 3)
    return k


def program(nc, a, out):
    with ExitStack() as ctx:
        k = setup(nc, ctx)
        attention(nc, k, a["x"], a["L0_attn_Wq"], a["L0_attn_bq"], a["L0_attn_Wk"], a["L0_attn_bk"],
                  a["L0_attn_Wv"], a["L0_attn_bv"], a["L0_attn_Wo"], a["L0_attn_bo"], a["L0_attn_sample_idx"])
        k.CWT = ctx.enter_context(nc.sbuf_tensor("CWT", [P, NCH * CW], BF16))
        gated_experts(nc, k, a["ctx_512"], a["itok_BxS2xS_0_7"], a["w_in"], a["w_out"], a["L0_ffn_Wr"])
        routed_experts(nc, k, a["w_gate"], a["w_up"], a["w_down"], out)


def kernel(**inputs):
    import numpy as np
    import concourse.bacc as bacc
    from concourse.bass_utils import run_bass_kernel_spmd as run

    v = {name: np.asarray(value) for name, value in inputs.items()}
    v["w_in"] = v.pop("L0_xattn_proj_in").transpose(2, 0, 1).reshape(D, U1, P)
    v["w_out"] = v.pop("L0_xattn_proj_out").reshape(E1, D, HID1 // P, P).transpose(3, 0, 2, 1).reshape(P, U1, D)
    for name, routed, shared in (("w_gate", "Wg", "Sg"), ("w_up", "Wu", "Su")):
        tiles = v.pop("L0_ffn_" + routed).transpose(1, 0, 2).reshape(D, U2 - 1, P)
        v[name] = np.concatenate([tiles, v.pop("L0_ffn_" + shared).reshape(D, 1, P)], axis=1)
    tiles = v.pop("L0_ffn_Wd").reshape(U2 - 1, P, D).transpose(1, 0, 2)
    v["w_down"] = np.concatenate([tiles, v.pop("L0_ffn_Sd").reshape(P, 1, D)], axis=1)

    nc = bacc.Bacc("TRN2", target_bir_lowering=False, num_devices=1)
    arrays, aps = {}, {}
    for name, value in v.items():
        arrays["in_" + name] = np.ascontiguousarray(value)
        aps[name] = nc.dram_tensor("in_" + name, value.shape, mybir.dt.from_np(value.dtype),
                                   kind="ExternalInput").ap()
    out = nc.dram_tensor("out", (B, L, D), F32, kind="ExternalOutput").ap()
    program(nc, aps, out)
    return run(nc, [arrays], core_ids=[0]).results[0]["out"]
```
